# Optimizing a Trainium2 kernel written in Bass

```python
import numpy as np
import jax
import jax.numpy as jnp

def _softmax(x, axis=-1):
    return jax.nn.softmax(x, axis=axis)

def _gelu(x):
    return jax.nn.gelu(x, approximate=True)

def _silu(x):
    return jax.nn.silu(x)

def _sigmoid(x):
    return jax.nn.sigmoid(x)

def _layernorm(x, axis=-1, eps=1e-05):
    m = jnp.mean(x, axis=axis, keepdims=True)
    v = jnp.var(x, axis=axis, keepdims=True)
    return (x - m) / jnp.sqrt(v + eps)

def _scatter_add(tgt, idx, src, axis=0):
    return tgt.at[idx].add(src)

def _segment_sum(src, seg, n):
    return jax.ops.segment_sum(src, seg, n)
kernel_name = 'mk_cond_seq_d1_seqx_r8_e76290'

def setup_inputs(seed: int=0):
    np.random.seed(seed)
    _w = jnp.asarray

    def _rec_inputs():
        import jax
        import jax.numpy as jnp
        _rk = jax.random.key(seed)
        x = -0.0003482 + 1 * jax.random.normal(jax.random.fold_in(_rk, 1), (8, 256, 144), jnp.float32)
        _lenS = 256 - jax.random.randint(jax.random.fold_in(_rk, 7), (8,), 0, max(1, 256 // 4) + 1, jnp.int32)
        _lenS2 = 256 - jax.random.randint(jax.random.fold_in(_rk, 8), (8,), 0, max(1, 256 // 4) + 1, jnp.int32)
        cond_1152 = 0.00257642 + 1.0011 * jax.random.normal(jax.random.fold_in(_rk, 11), (8, 144), jnp.float32)
        return (x, cond_1152)
    x, cond_1152 = _rec_inputs()

    def _L0_cond_setup():
        import jax, jax.numpy as jnp
        import numpy as np
        H = 144
        NH = 16
        HD = H // NH
        MLP = int(H * 4.0)
        EPS = 1e-06

        def _ln(z, scale=None):
            m = jnp.mean(z, axis=-1, keepdims=True)
            v = jnp.mean(jnp.square(z - m), axis=-1, keepdims=True)
            y = (z - m) * jax.lax.rsqrt(v + EPS)
            if scale is not None:
                y = y * scale
            return y
        key = jax.random.key(seed)
        ks = jax.random.split(key, 16)
        B, N = (16, 128)
        x = jax.random.normal(ks[0], (B, N, H), dtype=jnp.float32)
        c = jax.random.normal(ks[1], (B, H), dtype=jnp.float32)

        def xav(k, fan_in, fan_out):
            lim = np.sqrt(6.0 / (fan_in + fan_out))
            return jax.random.uniform(k, (fan_in, fan_out), jnp.float32, -lim, lim)
        w_mod = 0.02 * jax.random.normal(ks[2], (H, 6 * H), dtype=jnp.float32)
        b_mod = 0.02 * jax.random.normal(ks[3], (6 * H,), dtype=jnp.float32)
        w_qkv = xav(ks[4], H, 3 * H)
        b_qkv = jnp.zeros((3 * H,), jnp.float32)
        g_q = jnp.ones((HD,), jnp.float32)
        g_k = jnp.ones((HD,), jnp.float32)
        w_proj = xav(ks[5], H, H)
        b_proj = jnp.zeros((H,), jnp.float32)
        w1 = xav(ks[6], H, MLP)
        b1 = jnp.zeros((MLP,), jnp.float32)
        w2 = xav(ks[7], MLP, H)
        b2 = jnp.zeros((H,), jnp.float32)
        return dict(x=x, c=c, w_mod=w_mod, b_mod=b_mod, w_qkv=w_qkv, b_qkv=b_qkv, g_q=g_q, g_k=g_k, w_proj=w_proj, b_proj=b_proj, w1=w1, b1=b1, w2=w2, b2=b2)
    _L0_cond_all = _L0_cond_setup()
    _L0_cond_in = {k: v for k, v in _L0_cond_all.items() if k in ('w_mod', 'b_mod', 'w_qkv', 'b_qkv', 'g_q', 'g_k', 'w_proj', 'b_proj', 'w1', 'b1', 'w2', 'b2')}
    del _L0_cond_all
    return {'x': x, 'cond_1152': cond_1152, 'L0_cond_w_mod': _L0_cond_in['w_mod'], 'L0_cond_b_mod': _L0_cond_in['b_mod'], 'L0_cond_w_qkv': _L0_cond_in['w_qkv'], 'L0_cond_b_qkv': _L0_cond_in['b_qkv'], 'L0_cond_g_q': _L0_cond_in['g_q'], 'L0_cond_g_k': _L0_cond_in['g_k'], 'L0_cond_w_proj': _L0_cond_in['w_proj'], 'L0_cond_b_proj': _L0_cond_in['b_proj'], 'L0_cond_w1': _L0_cond_in['w1'], 'L0_cond_b1': _L0_cond_in['b1'], 'L0_cond_w2': _L0_cond_in['w2'], 'L0_cond_b2': _L0_cond_in['b2']}

def reference(x, cond_1152, L0_cond_w_mod, L0_cond_b_mod, L0_cond_w_qkv, L0_cond_b_qkv, L0_cond_g_q, L0_cond_g_k, L0_cond_w_proj, L0_cond_b_proj, L0_cond_w1, L0_cond_b1, L0_cond_w2, L0_cond_b2):
    import jax
    import jax.numpy as jnp

    def _L0_cond_ref(x, c, w_mod, b_mod, w_qkv, b_qkv, g_q, g_k, w_proj, b_proj, w1, b1, w2, b2):
        import jax, jax.numpy as jnp
        import numpy as np
        H = 144
        NH = 16
        HD = H // NH
        MLP = int(H * 4.0)
        EPS = 1e-06

        def _ln(z, scale=None):
            m = jnp.mean(z, axis=-1, keepdims=True)
            v = jnp.mean(jnp.square(z - m), axis=-1, keepdims=True)
            y = (z - m) * jax.lax.rsqrt(v + EPS)
            if scale is not None:
                y = y * scale
            return y
        B, N, _ = x.shape
        mod = jax.nn.swish(c) @ w_mod + b_mod
        sh_msa, sc_msa, g_msa, sh_mlp, sc_mlp, g_mlp = jnp.split(mod, 6, axis=1)
        xn = _ln(x) * (1 + sc_msa[:, None, :]) + sh_msa[:, None, :]
        qkv = xn @ w_qkv + b_qkv
        qkv = qkv.reshape(B, N, 3, NH, HD).transpose(2, 0, 3, 1, 4)
        q, k, v = (qkv[0], qkv[1], qkv[2])
        q = _ln(q, g_q)
        k = _ln(k, g_k)
        attn = jax.nn.softmax(jnp.einsum('bhqd,bhkd->bhqk', q, k) * HD ** (-0.5), axis=-1)
        o = jnp.einsum('bhqk,bhkd->bhqd', attn, v)
        o = o.transpose(0, 2, 1, 3).reshape(B, N, H) @ w_proj + b_proj
        x = x + g_msa[:, None, :] * o
        xn2 = _ln(x) * (1 + sc_mlp[:, None, :]) + sh_mlp[:, None, :]
        h = jax.nn.gelu(xn2 @ w1 + b1, approximate=True)
        x = x + g_mlp[:, None, :] * (h @ w2 + b2)
        return x
    x = _L0_cond_ref(x, cond_1152, L0_cond_w_mod, L0_cond_b_mod, L0_cond_w_qkv, L0_cond_b_qkv, L0_cond_g_q, L0_cond_g_k, L0_cond_w_proj, L0_cond_b_proj, L0_cond_w1, L0_cond_b1, L0_cond_w2, L0_cond_b2)
    return x

_drawn_inputs = setup_inputs


def setup_inputs(seed=0):
    import zlib

    import numpy as np

    out = dict(_drawn_inputs(seed))
    spreads = {'L0_cond_b_qkv': (0.0, 0.559),
     'L0_cond_g_q': (1.0, 0.6),
     'L0_cond_g_k': (1.0, 0.6),
     'L0_cond_b_proj': (0.0, 0.537),
     'L0_cond_b1': (0.0, 0.647),
     'L0_cond_b2': (0.0, 0.552)}
    factors = {'L0_cond_b_mod': 5.147, 'L0_cond_w_qkv': 2.849}
    for name, (base, spread) in spreads.items():
        noise = np.random.default_rng([zlib.crc32(name.encode()), seed]).standard_normal(out[name].shape)
        drawn = base * np.exp(spread * noise) if base else spread * noise
        out[name] = jnp.asarray(drawn.astype(out[name].dtype))
    for name, factor in factors.items():
        out[name] = (out[name] * factor).astype(out[name].dtype)
    return out
```

```python
from contextlib import ExitStack

import concourse.bass as bass
from concourse import mybir

F32 = mybir.dt.float32
F16 = mybir.dt.float16
I32 = mybir.dt.int32
ACT = mybir.ActivationFunctionType
ALU = mybir.AluOpType
AX = mybir.AxisListType
ds = bass.ds

B, N, H = 8, 256, 144
NH, HD = 16, 9
MLP = 4 * H
P = 128
I = N // P
QKV = 3 * H
EPS = 1e-6
JG = 4
SLOT = 32
NC = 4
CW = H // NC
KR = 3 * CW + 2
HT = H // 2
FT = 120
NF = 5
FW = [FT, FT, FT, FT, MLP - 4 * FT]
U = 8
XS, WS = 2.0 ** 4, 2.0 ** 8
QS = 2.0 ** 12
UNSCALE = 1.0 / (XS * WS)
SAFE_BOUND = 60.0
HALF_STEP = -0.5
MODS = 8
A1, A2, B1, B2, GA, GM, GAB, GMB = range(MODS)


class Steps:

    def __init__(self, sem, names):
        self.sem, self.names = sem, names.split()

    def after(self, b, name):
        return b * len(self.names) + (self.names.index(name) + 1)


class Prep:

    def __init__(self, sem, tag):
        self.pool = Steps(sem(tag + "_pool"), "z0 z1 za xm xg")
        self.gain = Steps(sem(tag + "_gain"), "sh qg")
        self.dve = Steps(sem(tag + "_dve"), "xhi xlo xT ssum n1 n2 rstd kn qn khi klo qhi qlo "
                         "qT0 qT1 qT2 qT3 qT4 qT5 qT6 qT7")
        self.act = Steps(sem(tag + "_act"), "sq v ln y0 kT")
        self.pe = Steps(sem(tag + "_pe"), "xT qkv kT qT")


def build(nc, x, cT, w_mod, b_mod, w_qkv, g_q, g_k, w_proj, b_proj, w1, w2, b2, ident, lo_rows, out):
    with ExitStack() as ctx:
        def sb(name, shape, dt=F32):
            return ctx.enter_context(nc.sbuf_tensor(name, shape, dt))

        def sem(name):
            return ctx.enter_context(nc.semaphore(name))

        id32 = sb("id32", [P, P])
        id16 = sb("id16", [P, P], F16)
        lo_row = sb("lo_row", [KR, 1])
        eps = sb("eps", [P, 1])
        c_sb = sb("c_sb", [HT, 2, B])
        c_e = sb("c_e", [HT, 2, B])
        c_s = sb("c_s", [HT, 2, B])
        bm_sb = sb("bm_sb", [B, 6 * H])
        bias2 = sb("bias2", [B, 2, H])
        mod = sb("mod", [B, 6 * H])
        mrow = sb("mrow", [B, MODS, H])
        mbc = sb("mbc", [P, B, MODS * H])
        gqk = sb("gqk", [P, 2, HD])
        gp = sb("gp", [P, HD])
        gneg = sb("gneg", [P, HD])
        gabs = sb("gabs", [P, HD])
        gmax = sb("gmax", [P, 1])
        gsafe = sb("gsafe", [P, 1])
        ginv = sb("ginv", [P, 1])
        gbc = sb("gbc", [P, NH, HD])
        escale = sb("escale", [P, 1])
        flagf = sb("flagf", [P, 1])
        flag = sb("flag", [P, 1], I32)
        wq_f = sb("wq_f", [KR, NC, QKV])
        wq_m = sb("wq_m", [KR, NC, 2 * NH])
        wq_h = sb("wq_h", [KR, NC, QKV], F16)
        wq = sb("wq", [KR, NC, QKV], F16)
        w1s = sb("w1s", [KR, NC, MLP], F16)
        w2_sb = sb("w2_sb", [FT, NF, H])
        wp_sb = sb("wp_sb", [HT, 2, H])

        xall = sb("xall", [P, B, I * H])
        bst = sb("bst", [P, B * I, 6])
        mv = sb("mv", [P, B * I, 2])
        ly = sb("ly", [P, B * I])
        y0 = sb("y0", [P, B * I])
        nt = sb("nt", [P, B * I])
        rstd = sb("rstd", [P, B * I])
        z = sb("z", [P, I, H])
        xa = sb("xa", [P, I, H])
        xm = sb("xm", [P, I, H])
        xst = sb("xst", [P, I * NC, P], F16)
        xT = sb("xT", [KR, NC, N], F16)
        sq = sb("sq", [P, I, 2 * H])
        ssum = sb("ssum", [P, I * 2 * NH])
        qly = sb("qly", [P, I * 2 * NH])
        qy0 = sb("qy0", [P, I * 2 * NH])
        qnt = sb("qnt", [P, I * 2 * NH])
        qrs = sb("qrs", [P, I * 2 * NH])
        qn = sb("qn", [P, I, H])
        kn = sb("kn", [P, I, H])
        qg = sb("qg", [P, I, H])
        qst = sb("qst", [P, I * NH, SLOT], F16)
        kst = sb("kst", [P, I * NH, SLOT], F16)
        v = [sb(f"v{i}", [P, I, NH, SLOT]) for i in range(2)]
        kT = [sb(f"kT{i}", [P, JG, N], F16) for i in range(2)]
        qT = [sb(f"qT{i}", [P, JG, 4, N], F16) for i in range(2)]
        shift = sb("shift", [P, B, I * NH * 3], F16)
        rmax = sb("rmax", [P, I * NH])
        sres = sb("sres", [P, I * NH])
        NP = 4
        pTs = sb("pTs", [P, NP, 4 * N])
        pT = [pTs[:, i, :].rearrange("p (g n) -> p g n", g=4) for i in range(NP)]
        wm_sb = pTs[0:HT].rearrange("p i n -> p (i n)")[:, 0:12 * H].rearrange("p (h n) -> p h n", h=2)
        oT = [sb(f"oT{i}", [P, JG, N]) for i in range(2)]
        rden = sb("rden", [P, I * NH])
        o_tok = sb("o_tok", [P, I * NH, HD])
        o_ch = sb("o_ch", [HT, 2, N])
        xt = sb("xt", [P, I, H])

        NB = B // 2
        T = 2 * I
        bst2 = sb("bst2", [P, I, 6])
        x1 = sb("x1", [P, I, H])
        mv2 = sb("mv2", [P, B * I, 2])
        ly2 = sb("ly2", [P, B * I])
        y2 = sb("y2", [P, B * I])
        nt2 = sb("nt2", [P, B * I])
        rstd2 = sb("rstd2", [P, B * I])
        z2 = sb("z2", [P, T, H])
        z2a = sb("z2a", [P, T, H])
        z2m = sb("z2m", [P, T, H])
        zst = sb("zst", [P, T * NC, P], F16)
        late = sb("late", [P, B * MODS * H])
        mflat = late[0:1, :].rearrange("p (b m) -> p b m", b=B)
        w1_f = late[0:KR, 0:NC * MLP].rearrange("p (c n) -> p c n", c=NC)
        w1_h = late[0:KR, NC * MLP:NC * MLP * 3 // 2].bitcast(F16).rearrange("p (c n) -> p c n", c=NC)
        at = 0
        hT, zT, yo = [], [], []
        for i in range(2):
            hT.append(late[0:FT, at:at + NF * T * P].rearrange("p (f n) -> p f n", f=NF))
            at += NF * T * P
            zT.append(late[0:KR, at:at + NC * T * P // 2].bitcast(F16).rearrange("p (c n) -> p c n", c=NC))
            at += NC * T * P // 2
            yo.append(late[:, at:at + T * H].rearrange("p (b n) -> p b n", b=2))
            at += T * H
        yg = late[:, at:at + T * H].rearrange("p (b n) -> p b n", b=2)

        ps_s = ctx.enter_context(nc.psum_tensor("ps_s", [P, 4, 512], F32))
        ps_o = ctx.enter_context(nc.psum_tensor("ps_o", [P, 2, 512], F32))
        ps_x = ctx.enter_context(nc.psum_tensor("ps_x", [P, 2, 512], F32))

        def bank16(i, c=4):
            return ps_x[:, i, :].bitcast(F16).rearrange("p (c n) -> p c n", c=c)

        ld_c, ld_wm, ld_x, ld_wq, ld_id, ld_g, ld_w, ld_w1, ld_b = (
            sem(s) for s in "ld_c ld_wm ld_x ld_wq ld_id ld_g ld_w ld_w1 ld_b".split())
        ld_flat = sem("ld_flat")
        zeroed = sem("zeroed")
        ones_set = sem("ones_set")
        mod_bc = sem("mod_bc")
        w1_made = sem("w1_made")
        set_dve = Steps(sem("set_dve"), "eps id16 gp gneg gabs gmax gsafe ginv gbc escale flagf flag c1 c2 c_s "
                        "mean centred wq_h wq mod mA mB mG mGB "
                        "n1 n2 rstd")
        stat = sem("stat")
        set_act = Steps(sem("set_act"), "c_e ln y0")
        set_pe = sem("set_pe")
        pre = Prep(sem, "pre")
        gen_pe = sem("gen_pe")
        gen_max = sem("gen_max")
        gen_dve = Steps(sem("gen_dve"), "s0 hi r1 mid r2 lo")
        prep = Prep(sem, "prep")
        scored = sem("scored")
        exped = sem("exped")
        summed = sem("summed")
        o_out = sem("o_out")
        post_pe = Steps(sem("post_pe"), "otok och proj")
        post_dve = Steps(sem("post_dve"), "rden o och xt x1 bn0 bn1 bs")
        kept = sem("kept")
        ln2_dve = Steps(sem("ln2_dve"), "z0 z1 z2 z3 za zm zhi zlo zT0 zT1")
        stat2 = sem("stat2")
        root_dve = Steps(sem("root_dve"), "n1 n2 rstd")
        root_act = Steps(sem("root_act"), "ln y0")
        ln2_pe = Steps(sem("ln2_pe"), "zT0 zT1")
        res_pool = sem("res_pool")
        hid_pe = sem("hid_pe")
        gelued = sem("gelued")
        y_pe = sem("y_pe")
        fin_dve = Steps(sem("fin_dve"), "yg0 yo0 yg1 yo1")
        stored = [sem(f"stored{i}") for i in range(2)]

        block = ctx.enter_context(nc.Block())

        def xb(b):
            return xall[:, ds(b, 1), :].rearrange("p o (i c) -> p (o i) c", i=I)

        def mb(b, k):
            return mbc[:, ds(b, 1), k * H:(k + 1) * H].broadcast_to([P, I, H])

        def is_later(b, S=prep):
            return S is prep and (not isinstance(b, int) or b > 0)

        def two_before(b):
            return not isinstance(b, int) or b > 1

        def needs_max(eng):
            eng.wait_ge(set_dve.sem, set_dve.after(0, "flag"))
            return eng.value_load(flag[0:1, 0:1], min_val=0, max_val=1)

        @block.sync
        def _(sp):
            sp.dma_start(c_sb[:], cT).then_inc(ld_c, 16)
            sp.dma_start(wm_sb, w_mod).then_inc(ld_wm, 16)
            sp.dma_start(xall[:], x.rearrange("b (p i) c -> p b (i c)", i=I)).then_inc(ld_x, 16)
            sp.dma_start(lo_row[:], lo_rows).then_inc(ld_wq, 16)
            sp.dma_start(w2_sb[:], w2).then_inc(ld_w, 16)
            sp.dma_start(wp_sb[:], w_proj).then_inc(ld_w, 16)
            sp.wait_ge(set_dve.sem, set_dve.after(0, "mGB"))
            sp.dma_start(mflat, mrow[:].rearrange("b m h -> b (m h)")).then_inc(ld_flat, 16)
            sp.wait_ge(mod_bc, B)
            sp.dma_start(w1_f, w1).then_inc(ld_w1, 16)
            for k in range(NB):
                sp.wait_ge(fin_dve.sem, fin_dve.after(k, "yo1"))
                sp.dma_start(out[2 * k:2 * k + 2].rearrange("b (p i) c -> p b (i c)", i=I),
                             yo[k % 2]).then_inc(stored[k % 2], 16)
            for i in range(2):
                sp.wait_ge(stored[i], 16 * NB // 2)

        @block.gpsimd
        def _(pool):
            for t in (xst, qst, kst, zst, shift):
                nc.gpsimd.memset(t[:].bitcast(F32), 0.0).then_inc(zeroed, 1)
            for i in range(2):
                nc.gpsimd.memset(v[i][:], 0.0).then_inc(zeroed, 1)
                nc.gpsimd.memset(qT[i][:].bitcast(F32), 0.0).then_inc(zeroed, 1)
            pool.wait_ge(zeroed, 9)
            nc.gpsimd.memset(xst[:, :, 3 * CW:KR], XS).then_inc(ones_set, 1)
            nc.gpsimd.memset(zst[:, :, 3 * CW:KR], XS).then_inc(ones_set, 1)
            nc.gpsimd.memset(kst[:, :, 3 * HD:3 * HD + 3], QS).then_inc(ones_set, 1)
            for i in range(2):
                nc.gpsimd.memset(v[i][:, :, :, HD:HD + 1], 1.0).then_inc(ones_set, 1)
            pool.wait_ge(ld_flat, 16)
            for b in range(B):
                nc.gpsimd.partition_broadcast(mbc[:, b, :], mflat[:, b, :], P).then_inc(mod_bc, 1)
            pool.wait_ge(set_dve.sem, set_dve.after(0, "rstd"))
            pool.wait_ge(mod_bc, B)

            def norm(b, S):
                if is_later(b, S):
                    pool.wait_ge(S.pool.sem, S.pool.after(b - 1, "za"))
                nc.gpsimd.tensor_tensor(z[:], xb(b), mv[:, ds(b * I, I), 0:1].broadcast_to([P, I, H]),
                                        ALU.subtract).then_inc(S.pool.sem, 1)
                pool.wait_ge(S.pool.sem, S.pool.after(b, "z0"))
                nc.gpsimd.tensor_tensor(z[:], z[:], rstd[:, ds(b * I, I)].unsqueeze(2).broadcast_to([P, I, H]),
                                        ALU.mult).then_inc(S.pool.sem, 1)
                if is_later(b, S):
                    pool.wait_ge(S.pool.sem, S.pool.after(b - 1, "xm"))
                pool.wait_ge(S.pool.sem, S.pool.after(b, "z1"))
                nc.gpsimd.tensor_tensor(xa[:], z[:], mb(b, A1), ALU.mult).then_inc(S.pool.sem, 1)
                pool.wait_ge(S.pool.sem, S.pool.after(b, "za"))
                if is_later(b, S):
                    pool.wait_ge(S.dve.sem, S.dve.after(b - 1, "xlo"))
                nc.gpsimd.tensor_tensor(xm[:], xa[:], mb(b, B1), ALU.add).then_inc(S.pool.sem, 1)
                if S is prep:
                    nc.gpsimd.tensor_tensor(xb(b), xb(b), mb(b, GAB), ALU.add).then_inc(S.pool.sem, 1)
                else:
                    nc.gpsimd.memset(z[:, 0, :], 0.0).then_inc(S.pool.sem, 1)

            def gains(b, S):
                if is_later(b, S):
                    pool.wait_ge(S.pe.sem, S.pe.after(b - 1, "qT"))
                nc.gpsimd.tensor_copy(qst[:, :, 3 * HD:3 * HD + 3],
                                      shift[:, ds(b, 1), :].rearrange("p o (t s) -> p (o t) s", s=3)
                                      ).then_inc(S.gain.sem, 1)
                pool.wait_ge(S.dve.sem, S.dve.after(b, "qn"))
                if is_later(b, S):
                    pool.wait_ge(S.dve.sem, S.dve.after(b - 1, "qlo"))
                nc.gpsimd.tensor_tensor(qg[:], qn[:], gbc[:].rearrange("p (o h) d -> p o (h d)", o=1)
                                        .broadcast_to([P, I, H]), ALU.mult).then_inc(S.gain.sem, 1)

            with pool.If(needs_max(pool) == 1):
                with pool.Fori(0, B) as b:
                    pool.wait_ge(gen_dve.sem, gen_dve.after(b - 1, "lo"))
                    norm(b, pre)
                    gains(b, pre)

            norm(0, prep)
            norm(1, prep)
            gains(0, prep)
            pool.wait_ge(ld_w1, 16)
            nc.gpsimd.tensor_scalar(w1_f, w1_f, WS, None, ALU.mult).then_inc(w1_made, 1)
            pool.wait_ge(w1_made, 1)
            nc.gpsimd.tensor_scalar(w1_h, w1_f, lo_row[:, 0:1], None, ALU.mult).then_inc(w1_made, 1)
            pool.wait_ge(w1_made, 2)
            nc.gpsimd.tensor_tensor(w1s[:], w1_f, w1_h, ALU.subtract).then_inc(w1_made, 1)

            def keep(n):
                pool.wait_ge(post_dve.sem, post_dve.after(n, "x1"))
                nc.gpsimd.tensor_copy(xb(n), x1[:]).then_inc(kept, 1)

            norm(2, prep)
            gains(1, prep)
            with pool.Fori(2, B - 1) as b:
                norm(b + 1, prep)
                gains(b, prep)
                keep(b - 2)
            gains(B - 1, prep)
            for n in range(B - 3, B):
                keep(n)

            pool.wait_ge(kept, B)
            for k in range(NB):
                pool.wait_ge(ln2_dve.sem, ln2_dve.after(k, "z3"))
                xk = xall[:, 2 * k:2 * k + 2, :].rearrange("p b (i c) -> p b i c", i=I)
                gk = mbc[:, 2 * k:2 * k + 2, GMB * H:(GMB + 1) * H].unsqueeze(2).broadcast_to([P, 2, I, H])
                nc.gpsimd.tensor_tensor(xk, xk, gk, ALU.add).then_inc(res_pool, 1)

        @block.scalar
        def _(act):
            act.dma_start(wq_f[:], w_qkv).then_inc(ld_wq, 16)
            act.dma_start(bm_sb[:], b_mod.rearrange("(o c) -> o c", o=1).broadcast_to([B, 6 * H])).then_inc(ld_b, 16)
            act.dma_start(bias2[:, 0, :], b_proj.rearrange("(o c) -> o c", o=1).broadcast_to([B, H])).then_inc(ld_b, 16)
            act.dma_start(bias2[:, 1, :], b2.rearrange("(o c) -> o c", o=1).broadcast_to([B, H])).then_inc(ld_b, 16)
            act.dma_start(gqk[:, 0, :], g_q.rearrange("(o c) -> o c", o=1).broadcast_to([P, HD])).then_inc(ld_g, 16)
            act.dma_start(gqk[:, 1, :], g_k.rearrange("(o c) -> o c", o=1).broadcast_to([P, HD])).then_inc(ld_g, 16)
            act.dma_start(id32[:], ident).then_inc(ld_id, 16)
            act.preload_act_table_set("natural_log_exp_and_others")
            act.wait_ge(ld_c, 16)
            nc.scalar.activation(c_e[:], c_sb[:], ACT.Exp, scale=-1.0).then_inc(set_act.sem, 1)
            act.wait_ge(set_dve.sem, set_dve.after(0, "eps"))
            act.wait_ge(stat, 2 * B * I)
            nc.scalar.activation(ly[:], mv[:, :, 1], ACT.Ln, bias=eps[:, 0:1]).then_inc(set_act.sem, 1)
            act.wait_ge(set_act.sem, set_act.after(0, "ln"))
            nc.scalar.activation(y0[:], ly[:], ACT.Exp, scale=-0.5).then_inc(set_act.sem, 1)

            def squares(b, S, par):
                act.wait_ge(S.pe.sem, S.pe.after(b, "qkv"))
                if is_later(b, S):
                    act.wait_ge(S.dve.sem, S.dve.after(b - 1, "ssum"))
                nc.scalar.activation(sq[:], ps_x[:, :, 0:2 * H], ACT.Square, scale=UNSCALE / 3.0).then_inc(S.act.sem, 1)
                if S is prep and two_before(b):
                    act.wait_ge(summed, (b - 1) * U)
                if S is pre or isinstance(b, int):
                    act.wait_ge(ones_set, 5)
                nc.scalar.activation(v[par][:, :, :, 0:HD],
                                     ps_x[:, :, 2 * H:3 * H].rearrange("p i (h d) -> p i h d", d=HD),
                                     ACT.Copy, scale=UNSCALE).then_inc(S.act.sem, 1)

            def roots(b, S):
                act.wait_ge(S.dve.sem, S.dve.after(b, "ssum"))
                nc.scalar.activation(qly[:], ssum[:], ACT.Ln, bias=eps[:, 0:1]).then_inc(S.act.sem, 1)
                act.wait_ge(S.act.sem, S.act.after(b, "ln"))
                if is_later(b, S):
                    act.wait_ge(S.dve.sem, S.dve.after(b - 1, "rstd"))
                nc.scalar.activation(qy0[:], qly[:], ACT.Exp, scale=-0.5).then_inc(S.act.sem, 1)

            def k_out(b, S, par):
                act.wait_ge(S.pe.sem, S.pe.after(b, "kT"))
                if S is prep and two_before(b):
                    act.wait_ge(scored, (b - 1) * U)
                nc.scalar.activation(kT[par][:], bank16(0), ACT.Copy).then_inc(S.act.sem, 1)

            with act.If(needs_max(act) == 1):
                with act.Fori(0, B) as b:
                    act.wait_ge(gen_dve.sem, gen_dve.after(b - 1, "lo"))
                    squares(b, pre, 0)
                    roots(b, pre)
                    k_out(b, pre, 0)

            squares(0, prep, 0)
            roots(0, prep)
            k_out(0, prep, 0)

            def exponentials(n, u):
                act.wait_ge(scored, n * U + u + 1)
                if is_later(n) or u >= NP:
                    act.wait_ge(summed, n * U + (u - NP + 1))
                nc.scalar.activation(pT[u % NP].rearrange("p g n -> p (g n)"),
                                     ps_s[:, 2 * (u % 2):2 * (u % 2) + 2, :].rearrange("p a n -> p (a n)"),
                                     ACT.Exp, scale=escale[:, 0:1]).then_inc(exped, 1)

            def output(n, j, par):
                act.wait_ge(summed, n * U + (2 * j + 2))
                nc.scalar.activation(oT[par][:, j, :], ps_o[:, j % 2, 0:N], ACT.Copy).then_inc(o_out, 1)

            def iteration(n, par, first=False, last=False):
                exponentials(n, 0)
                if not first:
                    output(n - 1, 3, 1 - par)
                exponentials(n, 1)
                exponentials(n, 2)
                if not last:
                    squares(n + 1, prep, 1 - par)
                output(n, 0, par)
                exponentials(n, 3)
                if not last:
                    roots(n + 1, prep)
                exponentials(n, 4)
                output(n, 1, par)
                exponentials(n, 5)
                exponentials(n, 6)
                output(n, 2, par)
                if not last:
                    k_out(n + 1, prep, 1 - par)
                exponentials(n, 7)

            iteration(0, 0, first=True)
            with act.Fori(0, B // 2 - 1) as it:
                iteration(it * 2 + 1, 1)
                iteration(it * 2 + 2, 0)
            iteration(B - 1, 1, last=True)
            output(B - 1, 3, 1)

            act.wait_ge(stat2, B * I)
            nc.scalar.activation(ly2[:], mv2[:, :, 1], ACT.Ln, bias=eps[:, 0:1]).then_inc(root_act.sem, 1)
            act.wait_ge(root_act.sem, root_act.after(0, "ln"))
            nc.scalar.activation(y2[:], ly2[:], ACT.Exp, scale=-0.5).then_inc(root_act.sem, 1)
            for k in range(NB):
                for f in range(NF):
                    act.wait_ge(hid_pe, NF * k + f + 1)
                    if k >= 2:
                        act.wait_ge(y_pe, 2 * (k - 1))
                    nc.scalar.activation(hT[k % 2][0:FW[f], f, :], ps_s[0:FW[f], (NF * k + f) % 4, :],
                                         ACT.Gelu_apprx_tanh, scale=UNSCALE).then_inc(gelued, 1)

        @block.vector
        def _(dve):
            D = set_dve

            def done(name):
                dve.wait_ge(D.sem, D.after(0, name))

            nc.vector.memset(eps[:], EPS).then_inc(D.sem, 1)
            dve.wait_ge(ld_id, 16)
            nc.vector.tensor_copy(id16[:], id32[:]).then_inc(D.sem, 1)
            dve.wait_ge(ld_g, 32)
            nc.vector.tensor_tensor(gp[:], gqk[:, 0, :], gqk[:, 1, :], ALU.mult).then_inc(D.sem, 1)
            done("gp")
            nc.vector.tensor_scalar(gneg[:], gp[:], -1.0, None, ALU.mult).then_inc(D.sem, 1)
            done("gneg")
            nc.vector.tensor_tensor(gabs[:], gp[:], gneg[:], ALU.max).then_inc(D.sem, 1)
            done("gabs")
            nc.vector.tensor_reduce(gmax[:], gabs[:], AX.X, ALU.max).then_inc(D.sem, 1)
            done("gmax")
            nc.vector.tensor_scalar(gsafe[:], gmax[:], 1e-30, None, ALU.max).then_inc(D.sem, 1)
            done("gsafe")
            nc.vector.reciprocal(ginv[:], gsafe[:]).then_inc(D.sem, 1)
            done("ginv")
            nc.vector.tensor_scalar(gbc[:], gp[:].unsqueeze(1).broadcast_to([P, NH, HD]), ginv[:, 0:1], None,
                                    ALU.mult).then_inc(D.sem, 1)
            nc.vector.tensor_scalar(escale[:], gsafe[:], 1.0 / (3.0 * QS * QS), None, ALU.mult).then_inc(D.sem, 1)
            nc.vector.tensor_scalar(flagf[:], gmax[:], SAFE_BOUND / 3.0, None, ALU.is_gt).then_inc(D.sem, 1)
            done("flagf")
            nc.vector.tensor_copy(flag[:], flagf[:]).then_inc(D.sem, 1)
            dve.wait_ge(set_act.sem, set_act.after(0, "c_e"))
            nc.vector.tensor_scalar(c_e[:], c_e[:], 1.0, None, ALU.add).then_inc(D.sem, 1)
            done("c1")
            nc.vector.reciprocal(c_s[:], c_e[:]).then_inc(D.sem, 1)
            done("c2")
            nc.vector.tensor_tensor(c_s[:], c_s[:], c_sb[:], ALU.mult).then_inc(D.sem, 1)
            dve.wait_ge(ld_wq, 32)
            wh = wq_f[:, :, 0:2 * H].rearrange("p c (h d) -> p c h d", d=HD)
            nc.vector.tensor_reduce(wq_m[:], wh, AX.X, ALU.add).then_inc(D.sem, 1)
            done("mean")
            nc.vector.scalar_tensor_tensor(wh, wq_m[:].unsqueeze(3).broadcast_to([KR, NC, 2 * NH, HD]), -1.0 / HD, wh,
                                           ALU.mult, ALU.add).then_inc(D.sem, 1)
            done("centred")
            nc.vector.tensor_scalar(wq_h[:], wq_f[:], WS, lo_row[:, 0:1], ALU.mult, ALU.mult).then_inc(D.sem, 1)
            done("wq_h")
            nc.vector.scalar_tensor_tensor(wq[:], wq_f[:], WS, wq_h[:], ALU.mult, ALU.subtract).then_inc(D.sem, 1)
            dve.wait_ge(set_pe, 1)
            dve.wait_ge(ld_b, 48)
            nc.vector.tensor_tensor(mod[:].rearrange("b (a n) -> b a n", a=2), ps_s[0:B, 0:2, 0:3 * H],
                                    bm_sb[:].rearrange("b (a n) -> b a n", a=2), ALU.add).then_inc(D.sem, 1)
            done("mod")
            m3 = mod[:].rearrange("b (a k h) -> b a k h", a=2, k=3)
            nc.vector.tensor_scalar(mrow[:, A1:A1 + 2, :], m3[:, :, 1, :], 1.0, XS, ALU.add, ALU.mult).then_inc(D.sem, 1)
            nc.vector.tensor_scalar(mrow[:, B1:B1 + 2, :], m3[:, :, 0, :], XS, None, ALU.mult).then_inc(D.sem, 1)
            nc.vector.tensor_copy(mrow[:, GA:GA + 2, :], m3[:, :, 2, :]).then_inc(D.sem, 1)
            nc.vector.tensor_tensor(mrow[:, GAB:GAB + 2, :], m3[:, :, 2, :], bias2[:], ALU.mult).then_inc(D.sem, 1)
            dve.wait_ge(ld_x, 16)
            xi = xall[:].rearrange("p b (i c) -> p (b i) c", i=I)
            for t in range(B * I):
                nc.vector.bn_stats(bst[:, t, :], xi[:, t, :]).then_inc(stat, 1)
            dve.wait_ge(stat, B * I)
            for t in range(B * I):
                nc.vector.bn_aggr(mv[:, t, :], bst[:, t, :]).then_inc(stat, 1)
            dve.wait_ge(set_act.sem, set_act.after(0, "y0"))
            newton(nc, dve, D, 0, nt, y0, mv[:, :, 1], rstd)

            def stack(b, S):
                dve.wait_ge(S.pool.sem, S.pool.after(b, "xm"))
                if is_later(b, S):
                    dve.wait_ge(S.pe.sem, S.pe.after(b - 1, "xT"))
                xc = xm[:].rearrange("p i (c w) -> p (i c) w", w=CW)
                slots = xst[:, :, 0:3 * CW].rearrange("p t (s w) -> p t s w", w=CW)
                if not is_later(b, S):
                    dve.wait_ge(ones_set, 5)
                nc.vector.tensor_copy(slots[:, :, 0:3:2, :], xc.unsqueeze(2).broadcast_to([P, I * NC, 2, CW])
                                      ).then_inc(S.dve.sem, 1)
                dve.wait_ge(S.dve.sem, S.dve.after(b, "xhi"))
                nc.vector.tensor_tensor(slots[:, :, 1, :], xc, slots[:, :, 0, :], ALU.subtract).then_inc(S.dve.sem, 1)

            def xT_out(b, S):
                dve.wait_ge(S.pe.sem, S.pe.after(b, "xT"))
                if is_later(b, S):
                    dve.wait_ge(S.pe.sem, S.pe.after(b - 1, "qkv"))
                nc.vector.tensor_copy(xT[:], bank16(0)[0:KR]).then_inc(S.dve.sem, 1)

            def norm_qk(b, S):
                dve.wait_ge(S.act.sem, S.act.after(b, "sq"))
                nc.vector.tensor_reduce(ssum[:], sq[:].rearrange("p i (h d) -> p (i h) d", d=HD), AX.X, ALU.add
                                        ).then_inc(S.dve.sem, 1)
                dve.wait_ge(S.act.sem, S.act.after(b, "y0"))
                newton(nc, dve, S.dve, b, qnt, qy0, ssum[:], qrs)
                dve.wait_ge(S.dve.sem, S.dve.after(b, "rstd"))
                r = qrs[:].rearrange("p (i k h) -> p i k h", i=I, k=2)
                for k, t in ((1, kn), (0, qn)):
                    if k == 0 and is_later(b, S):
                        dve.wait_ge(S.gain.sem, S.gain.after(b - 1, "qg"))
                    nc.vector.tensor_tensor(t[:].rearrange("p i (h d) -> p i h d", d=HD),
                                            ps_x[:, :, k * H:(k + 1) * H].rearrange("p i (h d) -> p i h d", d=HD),
                                            r[:, :, k, :].unsqueeze(3).broadcast_to([P, I, NH, HD]), ALU.mult
                                            ).then_inc(S.dve.sem, 1)
                if is_later(b, S):
                    dve.wait_ge(S.pe.sem, S.pe.after(b - 1, "kT"))
                dve.wait_ge(S.dve.sem, S.dve.after(b, "kn"))
                kh = kn[:].rearrange("p i (h d) -> p (i h) d", d=HD)
                slots = kst[:, :, 0:3 * HD].rearrange("p t (s d) -> p t s d", d=HD)
                nc.vector.tensor_copy(slots[:, :, 0:2, :], kh.unsqueeze(2).broadcast_to([P, I * NH, 2, HD])
                                      ).then_inc(S.dve.sem, 1)
                dve.wait_ge(S.dve.sem, S.dve.after(b, "khi"))
                nc.vector.tensor_tensor(slots[:, :, 2, :], kh, slots[:, :, 0, :], ALU.subtract).then_inc(S.dve.sem, 1)

            def split_q(b, S):
                dve.wait_ge(S.gain.sem, S.gain.after(b, "qg"))
                qh = qg[:].rearrange("p i (h d) -> p (i h) d", d=HD)
                slots = qst[:, :, 0:3 * HD].rearrange("p t (s d) -> p t s d", d=HD)
                nc.vector.tensor_copy(slots[:, :, 0:3:2, :], qh.unsqueeze(2).broadcast_to([P, I * NH, 2, HD])
                                      ).then_inc(S.dve.sem, 1)
                dve.wait_ge(S.dve.sem, S.dve.after(b, "qhi"))
                nc.vector.tensor_tensor(slots[:, :, 1, :], qh, slots[:, :, 0, :], ALU.subtract).then_inc(S.dve.sem, 1)

            def q_out(b, S, par):
                dve.wait_ge(S.pe.sem, S.pe.after(b, "qT"))
                if S is prep and two_before(b):
                    dve.wait_ge(scored, (b - 1) * U)
                for half in range(2):
                    for g in range(4):
                        rows = slice(SLOT * g, SLOT * (g + 1))
                        js = slice(2 * half, 2 * half + 2)
                        nc.vector.tensor_copy(qT[par][rows, js, g, :], bank16(1)[rows, js, :]).then_inc(S.dve.sem, 1)

            def maxima(b):
                for m in range(I * NH // 2):
                    dve.wait_ge(gen_pe, b * (I * NH // 2) + m + 1)
                    nc.vector.tensor_reduce(rmax[:, 2 * m:2 * m + 2], ps_x[:, m % 2, :].rearrange("p (h n) -> p h n", h=2),
                                            AX.X, ALU.max).then_inc(gen_max, 1)
                dve.wait_ge(gen_max, (b + 1) * (I * NH // 2))
                part = shift[:, ds(b, 1), :].rearrange("p o (t s) -> p (o t) s", s=3)
                nc.vector.tensor_scalar(sres[:], rmax[:], -1.0 / QS, None, ALU.mult).then_inc(gen_dve.sem, 1)
                for s, (name, made) in enumerate((("s0", "hi"), ("r1", "mid"), ("r2", "lo"))):
                    dve.wait_ge(gen_dve.sem, gen_dve.after(b, name))
                    nc.vector.tensor_copy(part[:, :, s], sres[:]).then_inc(gen_dve.sem, 1)
                    if s < 2:
                        dve.wait_ge(gen_dve.sem, gen_dve.after(b, made))
                        nc.vector.tensor_tensor(sres[:], sres[:], part[:, :, s], ALU.subtract).then_inc(gen_dve.sem, 1)

            with dve.If(needs_max(dve) == 1):
                with dve.Fori(0, B) as b:
                    stack(b, pre)
                    xT_out(b, pre)
                    norm_qk(b, pre)
                    split_q(b, pre)
                    q_out(b, pre, 0)
                    maxima(b)

            stack(0, prep)
            xT_out(0, prep)
            norm_qk(0, prep)
            split_q(0, prep)
            q_out(0, prep, 0)

            def normalise(n):
                dve.wait_ge(post_pe.sem, post_pe.after(n, "otok"))
                ot = ps_x[:].rearrange("p i (h s) -> p (i h) s", s=SLOT)
                nc.vector.reciprocal(rden[:], ot[:, :, HD]).then_inc(post_dve.sem, 1)
                dve.wait_ge(post_dve.sem, post_dve.after(n, "rden"))
                nc.vector.tensor_tensor(o_tok[:], ot[:, :, 0:HD], rden[:].unsqueeze(2).broadcast_to([P, I * NH, HD]),
                                        ALU.mult).then_inc(post_dve.sem, 1)

            def residual(n):
                dve.wait_ge(post_pe.sem, post_pe.after(n, "och"))
                nc.vector.tensor_copy(o_ch[:], ps_x[0:HT, 0, :].rearrange("p (c n) -> p c n", c=2)).then_inc(post_dve.sem, 1)
                dve.wait_ge(post_pe.sem, post_pe.after(n, "proj"))
                nc.vector.tensor_tensor(xt[:], ps_x[:, 1, 0:I * H].rearrange("p (i c) -> p i c", i=I), mb(n, GA),
                                        ALU.mult).then_inc(post_dve.sem, 1)
                dve.wait_ge(post_dve.sem, post_dve.after(n, "xt"))
                dve.wait_ge(prep.pool.sem, prep.pool.after(n, "xg"))
                dve.wait_ge(kept, n)
                nc.vector.tensor_tensor(x1[:], xb(n), xt[:], ALU.add).then_inc(post_dve.sem, 1)
                dve.wait_ge(post_dve.sem, post_dve.after(n, "x1"))
                for i in range(I):
                    nc.vector.bn_stats(bst2[:, i, :], x1[:, i, :]).then_inc(post_dve.sem, 1)
                dve.wait_ge(post_dve.sem, post_dve.after(n, "bn1"))
                nc.vector.tensor_copy(bst[:, ds(n * I, I), :], bst2[:]).then_inc(post_dve.sem, 1)

            def iteration(n, par, first=False, last=False):
                if not last:
                    stack(n + 1, prep)
                    xT_out(n + 1, prep)
                    norm_qk(n + 1, prep)
                if not first:
                    normalise(n - 1)
                if not last:
                    split_q(n + 1, prep)
                    q_out(n + 1, prep, 1 - par)
                if not first:
                    residual(n - 1)

            iteration(0, 0, first=True)
            with dve.Fori(0, B // 2 - 1) as it:
                iteration(it * 2 + 1, 1)
                iteration(it * 2 + 2, 0)
            iteration(B - 1, 1, last=True)
            normalise(B - 1)
            residual(B - 1)

            def norm2(k):
                L = ln2_dve

                def made(name, k=k):
                    dve.wait_ge(L.sem, L.after(k, name))

                xk = xall[:, 2 * k:2 * k + 2, :].rearrange("p b (i c) -> p (b i) c", i=I)
                for t in range(T):
                    nc.vector.tensor_scalar(z2[:, t, :], xk[:, t, :], mv2[:, T * k + t, 0:1],
                                            rstd2[:, T * k + t:T * k + t + 1],
                                            ALU.subtract, ALU.mult).then_inc(L.sem, 1)
                made("z3")

                def m2(r):
                    return mbc[:, 2 * k:2 * k + 2, r * H:(r + 1) * H].unsqueeze(2).broadcast_to([P, 2, I, H])

                def by_batch(t):
                    return t[:].rearrange("p (b i) c -> p b i c", i=I)

                nc.vector.tensor_tensor(by_batch(z2a), by_batch(z2), m2(A2), ALU.mult).then_inc(L.sem, 1)
                made("za")
                nc.vector.tensor_tensor(by_batch(z2m), by_batch(z2a), m2(B2), ALU.add).then_inc(L.sem, 1)
                made("zm")
                if k:
                    dve.wait_ge(ln2_pe.sem, ln2_pe.after(k - 1, "zT1"))
                zc = z2m[:].rearrange("p t (c w) -> p (t c) w", w=CW)
                slots = zst[:, :, 0:3 * CW].rearrange("p t (s w) -> p t s w", w=CW)
                nc.vector.tensor_copy(slots[:, :, 0:3:2, :], zc.unsqueeze(2).broadcast_to([P, T * NC, 2, CW])
                                      ).then_inc(L.sem, 1)
                made("zhi")
                nc.vector.tensor_tensor(slots[:, :, 1, :], zc, slots[:, :, 0, :], ALU.subtract).then_inc(L.sem, 1)
                for h in range(2):
                    dve.wait_ge(ln2_pe.sem, ln2_pe.after(k, f"zT{h}"))
                    if k >= 2:
                        dve.wait_ge(hid_pe, NF * (k - 1))
                    nc.vector.tensor_copy(zT[k % 2][:, 2 * h:2 * h + 2, :], bank16(h, 2)[0:KR]).then_inc(L.sem, 1)

            dve.wait_ge(post_dve.sem, post_dve.after(B - 1, "bs"))
            for t in range(B * I):
                nc.vector.bn_aggr(mv2[:, t, :], bst[:, t, :]).then_inc(stat2, 1)
            dve.wait_ge(kept, B)
            dve.wait_ge(root_act.sem, root_act.after(0, "y0"))
            newton(nc, dve, root_dve, 0, nt2, y2, mv2[:, :, 1], rstd2)
            dve.wait_ge(root_dve.sem, root_dve.after(0, "rstd"))
            norm2(0)
            for k in range(NB):
                if k + 1 < NB:
                    norm2(k + 1)
                dve.wait_ge(res_pool, k + 1)
                for n in range(2):
                    dve.wait_ge(y_pe, 2 * k + n + 1)
                    if k:
                        dve.wait_ge(fin_dve.sem, fin_dve.after(k - 1, f"yo{n}"))
                    b = 2 * k + n
                    nc.vector.tensor_tensor(yg[:, n, :].rearrange("p (i c) -> p i c", i=I),
                                            ps_o[:, n, 0:I * H].rearrange("p (i c) -> p i c", i=I), mb(b, GM),
                                            ALU.mult).then_inc(fin_dve.sem, 1)
                    dve.wait_ge(fin_dve.sem, fin_dve.after(k, f"yg{n}"))
                    if k >= 2:
                        dve.wait_ge(stored[k % 2], 16 * (k // 2))
                    nc.vector.tensor_tensor(yo[k % 2][:, n, :], yg[:, n, :], xall[:, b, :], ALU.add
                                            ).then_inc(fin_dve.sem, 1)

        @block.tensor
        def _(pe):
            pe.wait_ge(ld_wm, 16)
            pe.wait_ge(set_dve.sem, set_dve.after(0, "c_s"))
            for a in range(2):
                for h in range(2):
                    mm = nc.tensor.matmul(ps_s[0:B, a, 0:3 * H], c_s[:, h, :], wm_sb[:, h, a * 3 * H:(a + 1) * 3 * H],
                                          start=(h == 0), stop=(h == 1))
            mm.then_inc(set_pe, 1)
            pe.wait_ge(set_dve.sem, set_dve.after(0, "wq"))

            def transpose_x(b, S):
                pe.wait_ge(S.dve.sem, S.dve.after(b, "xlo"))
                for c in range(NC):
                    for i in range(I):
                        tr = nc.tensor.transpose(bank16(0)[0:KR, c, i * P:(i + 1) * P], xst[:, i * NC + c, 0:KR], id16[:])
                tr.then_inc(S.pe.sem, 1)

            def make_qkv(b, S):
                pe.wait_ge(S.dve.sem, S.dve.after(b, "xT"))
                for i in range(I):
                    for c in range(NC):
                        mm = nc.tensor.matmul(ps_x[:, i, 0:QKV], xT[:, c, i * P:(i + 1) * P], wq[:, c, :],
                                              start=(c == 0), stop=(c == NC - 1))
                mm.then_inc(S.pe.sem, 1)

            def transpose_heads(b, S, st, bank):
                for j in range(JG):
                    for i in range(I):
                        tr = nc.tensor.transpose(bank16(bank)[:, j, i * P:(i + 1) * P],
                                                 st[:, i * NH + 4 * j:i * NH + 4 * j + 4, :].rearrange("p h s -> p (h s)"),
                                                 id16[:])
                tr.then_inc(S.pe.sem, 1)

            def qkv_used(b, S):
                pe.wait_ge(S.act.sem, S.act.after(b, "v"))
                pe.wait_ge(S.dve.sem, S.dve.after(b, "qn"))

            def transpose_k(b, S):
                pe.wait_ge(S.dve.sem, S.dve.after(b, "klo"))
                transpose_heads(b, S, kst, 0)

            def transpose_q(b, S):
                pe.wait_ge(S.dve.sem, S.dve.after(b, "qlo"))
                pe.wait_ge(S.gain.sem, S.gain.after(b, "sh"))
                transpose_heads(b, S, qst, 1)

            with pe.If(needs_max(pe) == 1):
                with pe.Fori(0, B) as b:
                    pe.wait_ge(gen_dve.sem, gen_dve.after(b - 1, "lo"))
                    transpose_x(b, pre)
                    make_qkv(b, pre)
                    qkv_used(b, pre)
                    transpose_k(b, pre)
                    transpose_q(b, pre)
                    pe.wait_ge(pre.act.sem, pre.act.after(b, "kT"))
                    pe.wait_ge(pre.dve.sem, pre.dve.after(b, "qT7"))
                    for m in range(I * NH // 2):
                        if m >= 2:
                            pe.wait_ge(gen_max, b * (I * NH // 2) + (m - 1))
                        i, h = divmod(2 * m, NH)
                        for g in range(2):
                            j, r = divmod(h + g, 4)
                            mm = nc.tensor.matmul(ps_x[:, m % 2, g * N:(g + 1) * N], qT[0][:, j, r, i * P:(i + 1) * P],
                                                  kT[0][:, j, :], start=True, stop=True)
                        mm.then_inc(gen_pe, 1)

            transpose_x(0, prep)
            make_qkv(0, prep)
            qkv_used(0, prep)
            transpose_k(0, prep)
            transpose_q(0, prep)

            def scores(n, u, par):
                j, i = divmod(u, 2)
                if u == 0:
                    pe.wait_ge(prep.act.sem, prep.act.after(n, "kT"))
                    pe.wait_ge(prep.dve.sem, prep.dve.after(n, "qT3"))
                if u == 4:
                    pe.wait_ge(prep.dve.sem, prep.dve.after(n, "qT7"))
                if is_later(n) or u >= 2:
                    pe.wait_ge(exped, n * U + (u - 1))
                for a in range(2):
                    mm = nc.tensor.matmul(ps_s[:, 2 * (u % 2) + a, :], kT[par][:, j, i * P:(i + 1) * P],
                                          qT[par][:, j, 2 * a:2 * a + 2, :], start=True, stop=True)
                mm.then_inc(scored, 1)

            def values(n, u, par):
                j, i = divmod(u, 2)
                pe.wait_ge(exped, n * U + (u + 1))
                if i == 0 and (is_later(n) or j >= 2):
                    pe.wait_ge(o_out, n * JG + (j - 1))
                for g in range(4):
                    mm = nc.tensor.matmul(ps_o[SLOT * g:SLOT * (g + 1), j % 2, 0:N], v[par][:, i, 4 * j + g, :],
                                          pT[u % NP][:, g, :], start=(i == 0), stop=(i == I - 1))
                mm.then_inc(summed, 1)

            def transpose_o(n, par):
                pe.wait_ge(o_out, (n + 1) * JG)
                for i in range(I):
                    for j in range(JG):
                        tr = nc.tensor.transpose(ps_x[:, i, j * P:(j + 1) * P], oT[par][:, j, i * P:(i + 1) * P], id32[:])
                tr.then_inc(post_pe.sem, 1)

            def transpose_o_tok(n):
                pe.wait_ge(post_dve.sem, post_dve.after(n, "o"))
                ov = o_tok[:].rearrange("p (i h) d -> p i (h d)", i=I)
                for c in range(2):
                    for i in range(I):
                        tr = nc.tensor.transpose(ps_x[0:HT, 0, c * N + i * P:c * N + (i + 1) * P],
                                                 ov[:, i, c * HT:(c + 1) * HT], id32[:])
                tr.then_inc(post_pe.sem, 1)

            def project(n):
                pe.wait_ge(post_dve.sem, post_dve.after(n, "och"))
                for i in range(I):
                    for c in range(2):
                        mm = nc.tensor.matmul(ps_x[:, 1, i * H:(i + 1) * H], o_ch[:, c, i * P:(i + 1) * P], wp_sb[:, c, :],
                                              start=(c == 0), stop=(c == 1))
                mm.then_inc(post_pe.sem, 1)

            def iteration(n, par, first=False, last=False):
                scores(n, 0, par)
                if not last:
                    transpose_x(n + 1, prep)
                if not first:
                    values(n - 1, 7, 1 - par)
                scores(n, 1, par)
                if not last:
                    pe.wait_ge(prep.dve.sem, prep.dve.after(n + 1, "xlo"))
                    make_qkv(n + 1, prep)
                values(n, 0, par)
                for u in range(2, 4):
                    scores(n, u, par)
                    values(n, u - 1, par)
                scores(n, 4, par)
                if not last:
                    qkv_used(n + 1, prep)
                else:
                    pe.wait_ge(post_dve.sem, post_dve.after(n - 2, "xt"))
                if not first:
                    transpose_o(n - 1, 1 - par)
                values(n, 3, par)
                scores(n, 5, par)
                if not first:
                    pe.wait_ge(post_dve.sem, post_dve.after(n - 1, "o"))
                if not last:
                    transpose_k(n + 1, prep)
                values(n, 4, par)
                scores(n, 6, par)
                if not last:
                    transpose_q(n + 1, prep)
                values(n, 5, par)
                scores(n, 7, par)
                if not last:
                    pe.wait_ge(prep.act.sem, prep.act.after(n + 1, "kT"))
                if not first:
                    transpose_o_tok(n - 1)
                values(n, 6, par)
                if not first:
                    if not last:
                        pe.wait_ge(prep.dve.sem, prep.dve.after(n + 1, "qT7"))
                    project(n - 1)

            pe.wait_ge(ld_w, 32)
            iteration(0, 0, first=True)
            with pe.Fori(0, B // 2 - 1) as it:
                iteration(it * 2 + 1, 1)
                iteration(it * 2 + 2, 0)
            iteration(B - 1, 1, last=True)
            values(B - 1, 7, 1)
            pe.wait_ge(post_dve.sem, post_dve.after(B - 2, "xt"))
            transpose_o(B - 1, 1)
            transpose_o_tok(B - 1)
            project(B - 1)

            def transpose_z(k):
                pe.wait_ge(ln2_dve.sem, ln2_dve.after(k, "zlo"))
                if k == 0:
                    pe.wait_ge(post_dve.sem, post_dve.after(B - 1, "xt"))
                for h in range(2):
                    if k:
                        pe.wait_ge(ln2_dve.sem, ln2_dve.after(k - 1, f"zT{h}"))
                    for c in range(2):
                        for t in range(T):
                            tr = nc.tensor.transpose(bank16(h, 2)[0:KR, c, t * P:(t + 1) * P],
                                                     zst[:, t * NC + 2 * h + c, 0:KR], id16[:])
                    tr.then_inc(ln2_pe.sem, 1)

            transpose_z(0)
            pe.wait_ge(w1_made, 3)
            for k in range(NB):
                pe.wait_ge(ln2_dve.sem, ln2_dve.after(k, "zT1"))
                for f in range(NF):
                    m = NF * k + f
                    if m >= 4:
                        pe.wait_ge(gelued, m - 3)
                    for c in range(NC):
                        mm = nc.tensor.matmul(ps_s[0:FW[f], m % 4, :], w1s[:, c, f * FT:f * FT + FW[f]], zT[k % 2][:, c, :],
                                              start=(c == 0), stop=(c == NC - 1))
                    mm.then_inc(hid_pe, 1)
                if k + 1 < NB:
                    transpose_z(k + 1)
                pe.wait_ge(gelued, NF * (k + 1))
                for n in range(2):
                    if k:
                        pe.wait_ge(fin_dve.sem, fin_dve.after(k - 1, f"yg{n}"))
                    for i in range(I):
                        t = n * I + i
                        for f in range(NF):
                            mm = nc.tensor.matmul(ps_o[:, n, i * H:(i + 1) * H], hT[k % 2][0:FW[f], f, t * P:(t + 1) * P],
                                                  w2_sb[0:FW[f], f, :], start=(f == 0), stop=(f == NF - 1))
                    mm.then_inc(y_pe, 1)


def newton(nc, dve, steps, b, t, y, var, result):
    nc.vector.scalar_tensor_tensor(t[:], y[:], HALF_STEP, y[:], ALU.mult, ALU.mult).then_inc(steps.sem, 1)
    dve.wait_ge(steps.sem, steps.after(b, "n1"))
    nc.vector.scalar_tensor_tensor(t[:], var, EPS, t[:], ALU.add, ALU.mult).then_inc(steps.sem, 1)
    dve.wait_ge(steps.sem, steps.after(b, "n2"))
    nc.vector.scalar_tensor_tensor(result[:], t[:], 1.5, y[:], ALU.add, ALU.mult).then_inc(steps.sem, 1)


def kernel(**inputs):
    import numpy as np
    import concourse.bacc as bacc
    from concourse.bass_utils import run_bass_kernel_spmd

    def f(name):
        return np.ascontiguousarray(np.asarray(inputs[name]))

    def stacked(w, bias):
        n = w.shape[1]
        a = np.zeros((KR, NC, n), w.dtype)
        for s in range(3):
            a[s * CW:(s + 1) * CW] = w.reshape(NC, CW, n).transpose(1, 0, 2)
        a[3 * CW:, 0] = bias
        return a

    def halves(w):
        return np.ascontiguousarray(w.reshape(2, HT, -1).transpose(1, 0, 2))

    w2 = f("L0_cond_w2")
    w2p = np.zeros((NF * FT, H), w2.dtype)
    w2p[:MLP] = w2
    lo_rows = np.zeros((KR, 1), np.float32)
    lo_rows[2 * CW:3 * CW] = 1.0
    lo_rows[KR - 1] = 1.0
    arrays = {
        "x": f("x"),
        "cT": halves(f("cond_1152").T),
        "w_mod": halves(f("L0_cond_w_mod")),
        "b_mod": f("L0_cond_b_mod"),
        "w_qkv": stacked(f("L0_cond_w_qkv"), f("L0_cond_b_qkv")),
        "g_q": f("L0_cond_g_q"),
        "g_k": f("L0_cond_g_k"),
        "w_proj": halves(f("L0_cond_w_proj")),
        "b_proj": f("L0_cond_b_proj"),
        "w1": stacked(f("L0_cond_w1"), f("L0_cond_b1")),
        "w2": np.ascontiguousarray(w2p.reshape(NF, FT, H).transpose(1, 0, 2)),
        "b2": f("L0_cond_b2"),
        "ident": np.eye(P, dtype=np.float32),
        "lo_rows": lo_rows,
    }
    nc = bacc.Bacc("TRN2", target_bir_lowering=False, num_devices=1)
    args = [nc.dram_tensor("in_" + n, a.shape, mybir.dt.from_np(a.dtype), kind="ExternalInput").ap()
            for n, a in arrays.items()]
    out = nc.dram_tensor("out", (B, N, H), F32, kind="ExternalOutput").ap()
    build(nc, *args, out)
    r = run_bass_kernel_spmd(nc, [{"in_" + n: a for n, a in arrays.items()}], core_ids=[0])
    return r.results[0]["out"]
```

```python
from contextlib import ExitStack

import concourse.bass as bass
from concourse import mybir

F32 = mybir.dt.float32
F16 = mybir.dt.float16
I32 = mybir.dt.int32
ACT = mybir.ActivationFunctionType
ALU = mybir.AluOpType
AX = mybir.AxisListType
ds = bass.ds

B, N, H = 8, 256, 144
NH, HD = 16, 9
MLP = 4 * H
P = 128
I = N // P
QKV = 3 * H
EPS = 1e-6
JG = 4
SLOT = 32
NC = 4
CW = H // NC
KR = 3 * CW + 2
HT = H // 2
FT = 120
NF = 5
FW = [FT, FT, FT, FT, MLP - 4 * FT]
U = 8
XS, WS = 2.0 ** 4, 2.0 ** 8
QS = 2.0 ** 12
UNSCALE = 1.0 / (XS * WS)
SAFE_BOUND = 60.0
HALF_STEP = -0.5
MODS = 8
A1, A2, B1, B2, GA, GM, GAB, GMB = range(MODS)


class Steps:

    def __init__(self, sem, names):
        self.sem, self.names = sem, names.split()

    def after(self, b, name):
        return b * len(self.names) + (self.names.index(name) + 1)


class Prep:

    def __init__(self, sem, tag):
        self.pool = Steps(sem(tag + "_pool"), "z0 z1 za xm" + (" xg" if tag == "prep" else ""))
        self.gain = Steps(sem(tag + "_gain"), "sh qg")
        self.dve = Steps(sem(tag + "_dve"), "ssum n1 n2 rstd kn qn khi klo qhi qlo kT qT")
        self.wide = Steps(sem(tag + "_wide"), "g0 g1 g2 g3")
        self.x = Steps(sem(tag + "_x"), "xhi xlo xT")
        self.act = Steps(sem(tag + "_act"), "sq v ln y0")
        self.pe = Steps(sem(tag + "_pe"), "xT qkv kT qT")


def build(nc, x, cT, w_mod, b_mod, w_qkv, g_q, g_k, w_proj, b_proj, w1, w2, b2, ident, lo_rows, out):
    with ExitStack() as ctx:
        def sb(name, shape, dt=F32):
            return ctx.enter_context(nc.sbuf_tensor(name, shape, dt))

        def sem(name):
            return ctx.enter_context(nc.semaphore(name))

        id32 = sb("id32", [P, P])
        id16 = sb("id16", [P, P], F16)
        lo_row = sb("lo_row", [KR, 1])
        eps = sb("eps", [P, 1])
        c_sb = sb("c_sb", [HT, 2, B])
        c_e = sb("c_e", [HT, 2, B])
        c_s = sb("c_s", [HT, 2, B])
        bm_sb = sb("bm_sb", [B, 6 * H])
        bias2 = sb("bias2", [B, 2, H])
        mod = sb("mod", [B, 6 * H])
        mrow = sb("mrow", [B, MODS, H])
        mbc = sb("mbc", [P, B, MODS * H])
        gqk = sb("gqk", [P, 2, HD])
        gp = sb("gp", [P, HD])
        gneg = sb("gneg", [P, HD])
        gabs = sb("gabs", [P, HD])
        gmax = sb("gmax", [P, 1])
        gsafe = sb("gsafe", [P, 1])
        ginv = sb("ginv", [P, 1])
        gbc = sb("gbc", [P, NH, HD])
        escale = sb("escale", [P, 1])
        flagf = sb("flagf", [P, 1])
        flag = sb("flag", [P, 1], I32)
        wq_m = sb("wq_m", [KR, NC, 2 * NH])
        wq_h = sb("wq_h", [KR, NC, QKV], F16)
        wq = sb("wq", [KR, NC, QKV], F16)
        w1s = sb("w1s", [KR, NC, MLP], F16)
        w2_sb = sb("w2_sb", [FT, NF, H])
        wp_sb = sb("wp_sb", [HT, 2, H])

        xall = sb("xall", [P, B, I * H])
        bst = sb("bst", [P, B * I, 6])
        mv = sb("mv", [P, B * I, 2])
        ly = sb("ly", [P, B * I])
        y0 = sb("y0", [P, B * I])
        nt = sb("nt", [P, B * I])
        rstd = sb("rstd", [P, B * I])
        z = sb("z", [P, I, H])
        xa = sb("xa", [P, I, H])
        xm = sb("xm", [P, I, H])
        xst = sb("xst", [P, I * NC, P], F16)
        xT = sb("xT", [KR, NC, N], F16)
        sq = sb("sq", [P, I, 2 * H])
        ssum = sb("ssum", [P, I * 2 * NH])
        qly = sb("qly", [P, I * 2 * NH])
        qy0 = sb("qy0", [P, I * 2 * NH])
        qnt = sb("qnt", [P, I * 2 * NH])
        qrs = sb("qrs", [P, I * 2 * NH])
        qn = sb("qn", [P, I, H])
        kn = sb("kn", [P, I, H])
        qg = sb("qg", [P, I, H])
        qst = sb("qst", [P, I * NH, SLOT], F16)
        kst = sb("kst", [P, I * NH, SLOT], F16)
        v = [sb(f"v{i}", [P, I, NH, SLOT]) for i in range(2)]
        qP = sb("qP", [P, JG, N], F16)
        kT = [sb(f"kT{i}", [P, JG, N], F16) for i in range(2)]
        qT = [sb(f"qT{i}", [P, JG, 4, N], F16) for i in range(2)]
        shift = sb("shift", [P, B, I * NH * 3], F16)
        rmax = sb("rmax", [P, I * NH])
        sres = sb("sres", [P, I * NH])
        NP = 4
        pTs = sb("pTs", [P, NP, 4 * N])
        pT = [pTs[:, i, :].rearrange("p (g n) -> p g n", g=4) for i in range(NP)]
        wm_sb = pTs[0:HT].rearrange("p i n -> p (i n)")[:, 0:12 * H].rearrange("p (h n) -> p h n", h=2)
        oT = [sb(f"oT{i}", [P, JG, N]) for i in range(2)]
        rden = sb("rden", [P, I * NH])
        o_tok = sb("o_tok", [P, I * NH, HD])
        o_ch = sb("o_ch", [HT, 2, N])
        xt = sb("xt", [P, I, H])

        NB = B // 2
        T = 2 * I
        bst2 = sb("bst2", [P, I, 6])
        x1 = sb("x1", [P, I, H])
        mv2 = sb("mv2", [P, B * I, 2])
        ly2 = sb("ly2", [P, B * I])
        y2 = sb("y2", [P, B * I])
        nt2 = sb("nt2", [P, B * I])
        rstd2 = sb("rstd2", [P, B * I])
        z2s = sb("z2s", [P, 3, T, H])
        z2, z2a, z2m = (z2s[:, i] for i in range(3))
        wq_f = z2s[0:KR].rearrange("p a t c -> p (a t c)").rearrange("p (c n) -> p c n", c=NC)
        zst = sb("zst", [P, T * NC, P], F16)
        late = sb("late", [P, B * MODS * H])
        mflat = late[0:1, :].rearrange("p (b m) -> p b m", b=B)
        w1_f = late[0:KR, 0:NC * MLP].rearrange("p (c n) -> p c n", c=NC)
        w1_h = late[0:KR, NC * MLP:NC * MLP * 3 // 2].bitcast(F16).rearrange("p (c n) -> p c n", c=NC)
        at = 0
        hT, zT, yo = [], [], []
        for i in range(2):
            hT.append(late[0:FT, at:at + NF * T * P].rearrange("p (f n) -> p f n", f=NF))
            at += NF * T * P
            zT.append(late[0:KR, at:at + NC * T * P // 2].bitcast(F16).rearrange("p (c n) -> p c n", c=NC))
            at += NC * T * P // 2
            yo.append(late[:, at:at + T * H].rearrange("p (b n) -> p b n", b=2))
            at += T * H
        yg = late[:, at:at + T * H].rearrange("p (b n) -> p b n", b=2)

        ps_s = ctx.enter_context(nc.psum_tensor("ps_s", [P, 4, 512], F32))
        ps_o = ctx.enter_context(nc.psum_tensor("ps_o", [P, 2, 512], F32))
        ps_x = ctx.enter_context(nc.psum_tensor("ps_x", [P, 2, 512], F32))

        def bank16(i, c=4):
            return ps_x[:, i, :].bitcast(F16).rearrange("p (c n) -> p c n", c=c)

        ld_c, ld_wm, ld_x, ld_wq, ld_id, ld_g, ld_w, ld_w1, ld_b = (
            sem(s) for s in "ld_c ld_wm ld_x ld_wq ld_id ld_g ld_w ld_w1 ld_b".split())
        ld_flat = sem("ld_flat")
        zeroed = sem("zeroed")
        ones_set = sem("ones_set")
        mod_bc = sem("mod_bc")
        w1_made = sem("w1_made")
        set_dve = Steps(sem("set_dve"), "eps id16 gp gneg gabs gmax gsafe ginv gbc escale flagf flag c1 c2 c_s "
                        "mean centred wq_h wq mod mA mB mG mGB "
                        "n1 n2 rstd")
        stat = sem("stat")
        set_act = Steps(sem("set_act"), "c_e ln y0")
        set_pe = sem("set_pe")
        pre = Prep(sem, "pre")
        gen_pe = sem("gen_pe")
        gen_max = sem("gen_max")
        gen_dve = Steps(sem("gen_dve"), "s0 hi r1 mid r2 lo")
        prep = Prep(sem, "prep")
        scored = sem("scored")
        exped = sem("exped")
        summed = sem("summed")
        o_out = sem("o_out")
        post_pe = Steps(sem("post_pe"), "otok och proj")
        post_dve = Steps(sem("post_dve"), "rden o och x1 bn0 bn1 bs")
        gated = sem("gated")
        kept = sem("kept")
        ln2_dve = Steps(sem("ln2_dve"), "z0 z1 z2 z3 za zm zhi zlo zT0 zT1")
        stat2 = sem("stat2")
        root_dve = Steps(sem("root_dve"), "n1 n2 rstd")
        root_act = Steps(sem("root_act"), "ln y0")
        ln2_pe = Steps(sem("ln2_pe"), "zT0 zT1")
        res_pool = sem("res_pool")
        hid_pe = sem("hid_pe")
        gelued = sem("gelued")
        y_pe = sem("y_pe")
        fin_dve = Steps(sem("fin_dve"), "yg0 yo0 yg1 yo1")
        stored = [sem(f"stored{i}") for i in range(2)]

        block = ctx.enter_context(nc.Block())

        def xb(b):
            return xall[:, ds(b, 1), :].rearrange("p o (i c) -> p (o i) c", i=I)

        def mb(b, k):
            return mbc[:, ds(b, 1), k * H:(k + 1) * H].broadcast_to([P, I, H])

        def is_later(b, S=prep):
            return S is prep and (not isinstance(b, int) or b > 0)

        def two_before(b):
            return not isinstance(b, int) or b > 1

        def needs_max(eng):
            eng.wait_ge(set_dve.sem, set_dve.after(0, "flag"))
            return eng.value_load(flag[0:1, 0:1], min_val=0, max_val=1)

        @block.sync
        def _(sp):
            sp.dma_start(c_sb[:], cT).then_inc(ld_c, 16)
            sp.dma_start(wm_sb, w_mod).then_inc(ld_wm, 16)
            sp.dma_start(xall[:], x.rearrange("b (p i) c -> p b (i c)", i=I)).then_inc(ld_x, 16)
            sp.dma_start(lo_row[:], lo_rows).then_inc(ld_wq, 16)
            sp.dma_start(w2_sb[:], w2).then_inc(ld_w, 16)
            sp.dma_start(wp_sb[:], w_proj).then_inc(ld_w, 16)
            sp.wait_ge(set_dve.sem, set_dve.after(0, "mGB"))
            sp.dma_start(mflat, mrow[:].rearrange("b m h -> b (m h)")).then_inc(ld_flat, 16)
            for k in range(NB):
                sp.wait_ge(fin_dve.sem, fin_dve.after(k, "yo1"))
                sp.dma_start(out[2 * k:2 * k + 2].rearrange("b (p i) c -> p b (i c)", i=I),
                             yo[k % 2]).then_inc(stored[k % 2], 16)
            for i in range(2):
                sp.wait_ge(stored[i], 16 * NB // 2)

        @block.gpsimd
        def _(pool):
            for t in (xst, qst, kst, zst, shift):
                nc.gpsimd.memset(t[:].bitcast(F32), 0.0).then_inc(zeroed, 1)
            for i in range(2):
                nc.gpsimd.memset(v[i][:], 0.0).then_inc(zeroed, 1)
                nc.gpsimd.memset(qT[i][:].bitcast(F32), 0.0).then_inc(zeroed, 1)
            pool.wait_ge(zeroed, 9)
            nc.gpsimd.memset(xst[:, :, 3 * CW:KR], XS).then_inc(ones_set, 1)
            nc.gpsimd.memset(zst[:, :, 3 * CW:KR], XS).then_inc(ones_set, 1)
            nc.gpsimd.memset(kst[:, :, 3 * HD:3 * HD + 3], QS).then_inc(ones_set, 1)
            for i in range(2):
                nc.gpsimd.memset(v[i][:, :, :, HD:HD + 1], 1.0).then_inc(ones_set, 1)
            pool.wait_ge(ld_flat, 16)
            for b in range(B):
                nc.gpsimd.partition_broadcast(mbc[:, b, :], mflat[:, b, :], P).then_inc(mod_bc, 1)
            pool.wait_ge(mod_bc, B)
            pool.dma_start(w1_f, w1).then_inc(ld_w1, 16)
            pool.wait_ge(set_dve.sem, set_dve.after(0, "rstd"))

            def norm(b, S):
                if is_later(b, S):
                    pool.wait_ge(S.pool.sem, S.pool.after(b - 1, "za"))
                nc.gpsimd.tensor_tensor(z[:], xb(b), mv[:, ds(b * I, I), 0:1].broadcast_to([P, I, H]),
                                        ALU.subtract).then_inc(S.pool.sem, 1)
                pool.wait_ge(S.pool.sem, S.pool.after(b, "z0"))
                nc.gpsimd.tensor_tensor(z[:], z[:], rstd[:, ds(b * I, I)].unsqueeze(2).broadcast_to([P, I, H]),
                                        ALU.mult).then_inc(S.pool.sem, 1)
                if is_later(b, S):
                    pool.wait_ge(S.pool.sem, S.pool.after(b - 1, "xm"))
                pool.wait_ge(S.pool.sem, S.pool.after(b, "z1"))
                nc.gpsimd.tensor_tensor(xa[:], z[:], mb(b, A1), ALU.mult).then_inc(S.pool.sem, 1)
                pool.wait_ge(S.pool.sem, S.pool.after(b, "za"))
                if is_later(b, S):
                    pool.wait_ge(S.x.sem, S.x.after(b - 1, "xlo"))
                nc.gpsimd.tensor_tensor(xm[:], xa[:], mb(b, B1), ALU.add).then_inc(S.pool.sem, 1)

            def bias_in(b):
                nc.gpsimd.tensor_tensor(xb(b), xb(b), mb(b, GAB), ALU.add).then_inc(prep.pool.sem, 1)

            def gains(b, S):
                if is_later(b, S):
                    pool.wait_ge(S.pe.sem, S.pe.after(b - 1, "qT"))
                nc.gpsimd.tensor_copy(qst[:, :, 3 * HD:3 * HD + 3],
                                      shift[:, ds(b, 1), :].rearrange("p o (t s) -> p (o t) s", s=3)
                                      ).then_inc(S.gain.sem, 1)
                pool.wait_ge(S.dve.sem, S.dve.after(b, "qn"))
                if is_later(b, S):
                    pool.wait_ge(S.dve.sem, S.dve.after(b - 1, "qlo"))
                nc.gpsimd.tensor_tensor(qg[:], qn[:], gbc[:].rearrange("p (o h) d -> p o (h d)", o=1)
                                        .broadcast_to([P, I, H]), ALU.mult).then_inc(S.gain.sem, 1)

            with pool.If(needs_max(pool) == 1):
                with pool.Fori(0, B) as b:
                    pool.wait_ge(gen_dve.sem, gen_dve.after(b - 1, "lo"))
                    norm(b, pre)
                    gains(b, pre)
                pool.wait_ge(gen_dve.sem, gen_dve.after(B - 1, "lo"))

            norm(0, prep)
            bias_in(0)
            norm(1, prep)
            bias_in(1)
            gains(0, prep)
            pool.wait_ge(ld_w1, 16)
            nc.gpsimd.tensor_scalar(w1_f, w1_f, WS, None, ALU.mult).then_inc(w1_made, 1)
            pool.wait_ge(w1_made, 1)
            nc.gpsimd.tensor_scalar(w1_h, w1_f, lo_row[:, 0:1], None, ALU.mult).then_inc(w1_made, 1)
            pool.wait_ge(w1_made, 2)
            nc.gpsimd.tensor_tensor(w1s[:], w1_f, w1_h, ALU.subtract).then_inc(w1_made, 1)

            def keep(n):
                pool.wait_ge(post_dve.sem, post_dve.after(n, "x1"))
                nc.gpsimd.tensor_copy(xb(n), x1[:]).then_inc(kept, 1)

            norm(2, prep)
            gains(1, prep)
            bias_in(2)
            with pool.Fori(2, B - 1) as b:
                norm(b + 1, prep)
                gains(b, prep)
                bias_in(b + 1)
                keep(b - 2)
            gains(B - 1, prep)
            for n in range(B - 3, B):
                keep(n)

            pool.wait_ge(kept, B)
            for k in range(NB):
                pool.wait_ge(ln2_dve.sem, ln2_dve.after(k, "z3"))
                xk = xall[:, 2 * k:2 * k + 2, :].rearrange("p b (i c) -> p b i c", i=I)
                gk = mbc[:, 2 * k:2 * k + 2, GMB * H:(GMB + 1) * H].unsqueeze(2).broadcast_to([P, 2, I, H])
                nc.gpsimd.tensor_tensor(xk, xk, gk, ALU.add).then_inc(res_pool, 1)

        @block.scalar
        def _(act):
            act.dma_start(wq_f, w_qkv).then_inc(ld_wq, 16)
            act.dma_start(bm_sb[:], b_mod.rearrange("(o c) -> o c", o=1).broadcast_to([B, 6 * H])).then_inc(ld_b, 16)
            act.dma_start(bias2[:, 0, :], b_proj.rearrange("(o c) -> o c", o=1).broadcast_to([B, H])).then_inc(ld_b, 16)
            act.dma_start(bias2[:, 1, :], b2.rearrange("(o c) -> o c", o=1).broadcast_to([B, H])).then_inc(ld_b, 16)
            act.dma_start(gqk[:, 0, :], g_q.rearrange("(o c) -> o c", o=1).broadcast_to([P, HD])).then_inc(ld_g, 16)
            act.dma_start(gqk[:, 1, :], g_k.rearrange("(o c) -> o c", o=1).broadcast_to([P, HD])).then_inc(ld_g, 16)
            act.dma_start(id32[:], ident).then_inc(ld_id, 16)
            act.preload_act_table_set("natural_log_exp_and_others")
            act.wait_ge(ld_c, 16)
            nc.scalar.activation(c_e[:], c_sb[:], ACT.Exp, scale=-1.0).then_inc(set_act.sem, 1)
            act.wait_ge(set_dve.sem, set_dve.after(0, "eps"))
            act.wait_ge(stat, 2 * B * I)
            nc.scalar.activation(ly[:], mv[:, :, 1], ACT.Ln, bias=eps[:, 0:1]).then_inc(set_act.sem, 1)
            act.wait_ge(set_act.sem, set_act.after(0, "ln"))
            nc.scalar.activation(y0[:], ly[:], ACT.Exp, scale=-0.5).then_inc(set_act.sem, 1)

            def squares(b, S):
                act.wait_ge(S.pe.sem, S.pe.after(b, "qkv"))
                if is_later(b, S):
                    act.wait_ge(S.dve.sem, S.dve.after(b - 1, "ssum"))
                nc.scalar.activation(sq[:], ps_x[:, :, 0:2 * H], ACT.Square, scale=UNSCALE / 3.0).then_inc(S.act.sem, 1)

            def roots(b, S):
                act.wait_ge(S.dve.sem, S.dve.after(b, "ssum"))
                nc.scalar.activation(qly[:], ssum[:], ACT.Ln, bias=eps[:, 0:1]).then_inc(S.act.sem, 1)
                act.wait_ge(S.act.sem, S.act.after(b, "ln"))
                if is_later(b, S):
                    act.wait_ge(S.dve.sem, S.dve.after(b - 1, "rstd"))
                nc.scalar.activation(qy0[:], qly[:], ACT.Exp, scale=-0.5).then_inc(S.act.sem, 1)

            def v_out(b, S, par):
                if S is prep and two_before(b):
                    act.wait_ge(summed, (b - 1) * U)
                if S is pre or isinstance(b, int):
                    act.wait_ge(ones_set, 5)
                nc.scalar.activation(v[par][:, :, :, 0:HD],
                                     ps_x[:, :, 2 * H:3 * H].rearrange("p i (h d) -> p i h d", d=HD),
                                     ACT.Copy, scale=UNSCALE).then_inc(S.act.sem, 1)

            with act.If(needs_max(act) == 1):
                with act.Fori(0, B) as b:
                    act.wait_ge(gen_dve.sem, gen_dve.after(b - 1, "lo"))
                    squares(b, pre)
                    v_out(b, pre, 0)
                    roots(b, pre)
                act.wait_ge(gen_dve.sem, gen_dve.after(B - 1, "lo"))

            squares(0, prep)
            v_out(0, prep, 0)
            roots(0, prep)

            def exponentials(n, u):
                act.wait_ge(scored, n * U + u + 1)
                if is_later(n) or u >= NP:
                    act.wait_ge(summed, n * U + (u - NP + 1))
                nc.scalar.activation(pT[u % NP].rearrange("p g n -> p (g n)"),
                                     ps_s[:, 2 * (u % 2):2 * (u % 2) + 2, :].rearrange("p a n -> p (a n)"),
                                     ACT.Exp, scale=escale[:, 0:1]).then_inc(exped, 1)

            def output(n, j, par):
                act.wait_ge(summed, n * U + (2 * j + 2))
                nc.scalar.activation(oT[par][:, j, :], ps_o[:, j % 2, 0:N], ACT.Copy).then_inc(o_out, 1)

            def iteration(n, par, first=False, last=False):
                exponentials(n, 0)
                if not first:
                    output(n - 1, 3, 1 - par)
                exponentials(n, 1)
                if not last:
                    squares(n + 1, prep)
                    v_out(n + 1, prep, 1 - par)
                    roots(n + 1, prep)
                exponentials(n, 2)
                output(n, 0, par)
                exponentials(n, 3)
                exponentials(n, 4)
                output(n, 1, par)
                exponentials(n, 5)
                exponentials(n, 6)
                output(n, 2, par)
                exponentials(n, 7)

            iteration(0, 0, first=True)
            with act.Fori(0, B // 2 - 1) as it:
                iteration(it * 2 + 1, 1)
                iteration(it * 2 + 2, 0)
            iteration(B - 1, 1, last=True)
            output(B - 1, 3, 1)

            act.wait_ge(stat2, B * I)
            nc.scalar.activation(ly2[:], mv2[:, :, 1], ACT.Ln, bias=eps[:, 0:1]).then_inc(root_act.sem, 1)
            act.wait_ge(root_act.sem, root_act.after(0, "ln"))
            nc.scalar.activation(y2[:], ly2[:], ACT.Exp, scale=-0.5).then_inc(root_act.sem, 1)
            for k in range(NB):
                for f in range(NF):
                    act.wait_ge(hid_pe, NF * k + f + 1)
                    if k >= 2:
                        act.wait_ge(y_pe, 2 * (k - 1))
                    nc.scalar.activation(hT[k % 2][0:FW[f], f, :], ps_s[0:FW[f], (NF * k + f) % 4, :],
                                         ACT.Gelu_apprx_tanh, scale=UNSCALE).then_inc(gelued, 1)

        @block.vector
        def _(dve):
            D = set_dve

            def done(name):
                dve.wait_ge(D.sem, D.after(0, name))

            nc.vector.memset(eps[:], EPS).then_inc(D.sem, 1)
            dve.wait_ge(ld_id, 16)
            nc.vector.tensor_copy(id16[:], id32[:]).then_inc(D.sem, 1)
            dve.wait_ge(ld_g, 32)
            nc.vector.tensor_tensor(gp[:], gqk[:, 0, :], gqk[:, 1, :], ALU.mult).then_inc(D.sem, 1)
            done("gp")
            nc.vector.tensor_scalar(gneg[:], gp[:], -1.0, None, ALU.mult).then_inc(D.sem, 1)
            done("gneg")
            nc.vector.tensor_tensor(gabs[:], gp[:], gneg[:], ALU.max).then_inc(D.sem, 1)
            done("gabs")
            nc.vector.tensor_reduce(gmax[:], gabs[:], AX.X, ALU.max).then_inc(D.sem, 1)
            done("gmax")
            nc.vector.tensor_scalar(gsafe[:], gmax[:], 1e-30, None, ALU.max).then_inc(D.sem, 1)
            done("gsafe")
            nc.vector.reciprocal(ginv[:], gsafe[:]).then_inc(D.sem, 1)
            done("ginv")
            nc.vector.tensor_scalar(gbc[:], gp[:].unsqueeze(1).broadcast_to([P, NH, HD]), ginv[:, 0:1], None,
                                    ALU.mult).then_inc(D.sem, 1)
            nc.vector.tensor_scalar(escale[:], gsafe[:], 1.0 / (3.0 * QS * QS), None, ALU.mult).then_inc(D.sem, 1)
            nc.vector.tensor_scalar(flagf[:], gmax[:], SAFE_BOUND / 3.0, None, ALU.is_gt).then_inc(D.sem, 1)
            done("flagf")
            nc.vector.tensor_copy(flag[:], flagf[:]).then_inc(D.sem, 1)
            dve.wait_ge(set_act.sem, set_act.after(0, "c_e"))
            nc.vector.tensor_scalar(c_e[:], c_e[:], 1.0, None, ALU.add).then_inc(D.sem, 1)
            done("c1")
            nc.vector.reciprocal(c_s[:], c_e[:]).then_inc(D.sem, 1)
            done("c2")
            nc.vector.tensor_tensor(c_s[:], c_s[:], c_sb[:], ALU.mult).then_inc(D.sem, 1)
            dve.wait_ge(ld_wq, 32)
            wh = wq_f[:, :, 0:2 * H].rearrange("p c (h d) -> p c h d", d=HD)
            nc.vector.tensor_reduce(wq_m[:], wh, AX.X, ALU.add).then_inc(D.sem, 1)
            done("mean")
            nc.vector.scalar_tensor_tensor(wh, wq_m[:].unsqueeze(3).broadcast_to([KR, NC, 2 * NH, HD]), -1.0 / HD, wh,
                                           ALU.mult, ALU.add).then_inc(D.sem, 1)
            done("centred")
            nc.vector.tensor_scalar(wq_h[:], wq_f, WS, lo_row[:, 0:1], ALU.mult, ALU.mult).then_inc(D.sem, 1)
            done("wq_h")
            nc.vector.scalar_tensor_tensor(wq[:], wq_f, WS, wq_h[:], ALU.mult, ALU.subtract).then_inc(D.sem, 1)
            dve.wait_ge(set_pe, 1)
            dve.wait_ge(ld_b, 48)
            nc.vector.tensor_tensor(mod[:].rearrange("b (a n) -> b a n", a=2), ps_s[0:B, 0:2, 0:3 * H],
                                    bm_sb[:].rearrange("b (a n) -> b a n", a=2), ALU.add).then_inc(D.sem, 1)
            done("mod")
            m3 = mod[:].rearrange("b (a k h) -> b a k h", a=2, k=3)
            nc.vector.tensor_scalar(mrow[:, A1:A1 + 2, :], m3[:, :, 1, :], 1.0, XS, ALU.add, ALU.mult).then_inc(D.sem, 1)
            nc.vector.tensor_scalar(mrow[:, B1:B1 + 2, :], m3[:, :, 0, :], XS, None, ALU.mult).then_inc(D.sem, 1)
            nc.vector.tensor_copy(mrow[:, GA:GA + 2, :], m3[:, :, 2, :]).then_inc(D.sem, 1)
            nc.vector.tensor_tensor(mrow[:, GAB:GAB + 2, :], m3[:, :, 2, :], bias2[:], ALU.mult).then_inc(D.sem, 1)
            dve.wait_ge(ld_x, 16)
            xi = xall[:].rearrange("p b (i c) -> p (b i) c", i=I)
            for t in range(B * I):
                nc.vector.bn_stats(bst[:, t, :], xi[:, t, :]).then_inc(stat, 1)
            dve.wait_ge(stat, B * I)
            for t in range(B * I):
                nc.vector.bn_aggr(mv[:, t, :], bst[:, t, :]).then_inc(stat, 1)
            dve.wait_ge(set_act.sem, set_act.after(0, "y0"))
            newton(nc, dve, D, 0, nt, y0, mv[:, :, 1], rstd)

            def stack(b, S):
                dve.wait_ge(S.pool.sem, S.pool.after(b, "xm"))
                if is_later(b, S):
                    dve.wait_ge(S.pe.sem, S.pe.after(b - 1, "xT"))
                xc = xm[:].rearrange("p i (c w) -> p (i c) w", w=CW)
                slots = xst[:, :, 0:3 * CW].rearrange("p t (s w) -> p t s w", w=CW)
                if not is_later(b, S):
                    dve.wait_ge(ones_set, 5)
                nc.vector.tensor_copy(slots[:, :, 0:3:2, :], xc.unsqueeze(2).broadcast_to([P, I * NC, 2, CW])
                                      ).then_inc(S.x.sem, 1)
                dve.wait_ge(S.x.sem, S.x.after(b, "xhi"))
                nc.vector.tensor_tensor(slots[:, :, 1, :], xc, slots[:, :, 0, :], ALU.subtract).then_inc(S.x.sem, 1)

            def xT_out(b, S):
                dve.wait_ge(S.pe.sem, S.pe.after(b, "xT"))
                if is_later(b, S):
                    dve.wait_ge(S.pe.sem, S.pe.after(b - 1, "qkv"))
                nc.vector.tensor_copy(xT[:], bank16(1)[0:KR]).then_inc(S.x.sem, 1)

            def norm_qk(b, S):
                dve.wait_ge(S.act.sem, S.act.after(b, "sq"))
                nc.vector.tensor_reduce(ssum[:], sq[:].rearrange("p i (h d) -> p (i h) d", d=HD), AX.X, ALU.add
                                        ).then_inc(S.dve.sem, 1)
                dve.wait_ge(S.act.sem, S.act.after(b, "y0"))
                newton(nc, dve, S.dve, b, qnt, qy0, ssum[:], qrs)
                dve.wait_ge(S.dve.sem, S.dve.after(b, "rstd"))
                r = qrs[:].rearrange("p (i k h) -> p i k h", i=I, k=2)
                for k, t in ((1, kn), (0, qn)):
                    if k == 0 and is_later(b, S):
                        dve.wait_ge(S.gain.sem, S.gain.after(b - 1, "qg"))
                    nc.vector.tensor_tensor(t[:].rearrange("p i (h d) -> p i h d", d=HD),
                                            ps_x[:, :, k * H:(k + 1) * H].rearrange("p i (h d) -> p i h d", d=HD),
                                            r[:, :, k, :].unsqueeze(3).broadcast_to([P, I, NH, HD]), ALU.mult
                                            ).then_inc(S.dve.sem, 1)
                if is_later(b, S):
                    dve.wait_ge(S.pe.sem, S.pe.after(b - 1, "kT"))
                dve.wait_ge(S.dve.sem, S.dve.after(b, "kn"))
                kh = kn[:].rearrange("p i (h d) -> p (i h) d", d=HD)
                slots = kst[:, :, 0:3 * HD].rearrange("p t (s d) -> p t s d", d=HD)
                nc.vector.tensor_copy(slots[:, :, 0:2, :], kh.unsqueeze(2).broadcast_to([P, I * NH, 2, HD])
                                      ).then_inc(S.dve.sem, 1)
                dve.wait_ge(S.dve.sem, S.dve.after(b, "khi"))
                nc.vector.tensor_tensor(slots[:, :, 2, :], kh, slots[:, :, 0, :], ALU.subtract).then_inc(S.dve.sem, 1)

            def split_q(b, S):
                dve.wait_ge(S.gain.sem, S.gain.after(b, "qg"))
                qh = qg[:].rearrange("p i (h d) -> p (i h) d", d=HD)
                slots = qst[:, :, 0:3 * HD].rearrange("p t (s d) -> p t s d", d=HD)
                nc.vector.tensor_copy(slots[:, :, 0:3:2, :], qh.unsqueeze(2).broadcast_to([P, I * NH, 2, HD])
                                      ).then_inc(S.dve.sem, 1)
                dve.wait_ge(S.dve.sem, S.dve.after(b, "qhi"))
                nc.vector.tensor_tensor(slots[:, :, 1, :], qh, slots[:, :, 0, :], ALU.subtract).then_inc(S.dve.sem, 1)

            def k_out(b, S, par):
                dve.wait_ge(S.pe.sem, S.pe.after(b, "kT"))
                if S is prep and two_before(b):
                    dve.wait_ge(scored, (b - 1) * U)
                nc.vector.tensor_copy(kT[par][:], bank16(0)).then_inc(S.dve.sem, 1)

            def q_out(b, S):
                dve.wait_ge(S.pe.sem, S.pe.after(b, "qT"))
                if is_later(b, S):
                    dve.wait_ge(S.wide.sem, S.wide.after(b - 1, "g3"))
                nc.vector.tensor_copy(qP[:], bank16(1)).then_inc(S.dve.sem, 1)

            def widen(b, S, par):
                dve.wait_ge(S.dve.sem, S.dve.after(b, "qT"))
                if S is prep and two_before(b):
                    dve.wait_ge(scored, (b - 1) * U)
                for g in range(4):
                    rows = slice(SLOT * g, SLOT * (g + 1))
                    nc.vector.tensor_copy(qT[par][rows, :, g, :], qP[rows]).then_inc(S.wide.sem, 1)

            def maxima(b):
                for m in range(I * NH // 2):
                    dve.wait_ge(gen_pe, b * (I * NH // 2) + m + 1)
                    nc.vector.tensor_reduce(rmax[:, 2 * m:2 * m + 2], ps_x[:, m % 2, :].rearrange("p (h n) -> p h n", h=2),
                                            AX.X, ALU.max).then_inc(gen_max, 1)
                dve.wait_ge(gen_max, (b + 1) * (I * NH // 2))
                part = shift[:, ds(b, 1), :].rearrange("p o (t s) -> p (o t) s", s=3)
                nc.vector.tensor_scalar(sres[:], rmax[:], -1.0 / QS, None, ALU.mult).then_inc(gen_dve.sem, 1)
                for s, (name, made) in enumerate((("s0", "hi"), ("r1", "mid"), ("r2", "lo"))):
                    dve.wait_ge(gen_dve.sem, gen_dve.after(b, name))
                    nc.vector.tensor_copy(part[:, :, s], sres[:]).then_inc(gen_dve.sem, 1)
                    if s < 2:
                        dve.wait_ge(gen_dve.sem, gen_dve.after(b, made))
                        nc.vector.tensor_tensor(sres[:], sres[:], part[:, :, s], ALU.subtract).then_inc(gen_dve.sem, 1)

            with dve.If(needs_max(dve) == 1):
                with dve.Fori(0, B) as b:
                    stack(b, pre)
                    xT_out(b, pre)
                    norm_qk(b, pre)
                    split_q(b, pre)
                    k_out(b, pre, 0)
                    q_out(b, pre)
                    widen(b, pre, 0)
                    maxima(b)
                dve.wait_ge(gen_dve.sem, gen_dve.after(B - 1, "lo"))

            stack(0, prep)
            xT_out(0, prep)
            norm_qk(0, prep)
            split_q(0, prep)
            k_out(0, prep, 0)
            q_out(0, prep)
            widen(0, prep, 0)
            stack(1, prep)
            xT_out(1, prep)

            def normalise(n):
                dve.wait_ge(post_pe.sem, post_pe.after(n, "otok"))
                ot = ps_x[:].rearrange("p i (h s) -> p (i h) s", s=SLOT)
                nc.vector.reciprocal(rden[:], ot[:, :, HD]).then_inc(post_dve.sem, 1)
                dve.wait_ge(post_dve.sem, post_dve.after(n, "rden"))
                nc.vector.tensor_tensor(o_tok[:], ot[:, :, 0:HD], rden[:].unsqueeze(2).broadcast_to([P, I * NH, HD]),
                                        ALU.mult).then_inc(post_dve.sem, 1)

            def channels(n):
                dve.wait_ge(post_pe.sem, post_pe.after(n, "och"))
                nc.vector.tensor_copy(o_ch[:], ps_x[0:HT, 0, :].rearrange("p (c n) -> p c n", c=2)).then_inc(post_dve.sem, 1)

            def projected(n):
                dve.wait_ge(post_pe.sem, post_pe.after(n, "proj"))
                nc.vector.tensor_tensor(xt[:], ps_x[:, 0, 0:I * H].rearrange("p (i c) -> p i c", i=I), mb(n, GA),
                                        ALU.mult).then_inc(gated, 1)

            def residual(n):
                dve.wait_ge(gated, n + 1)
                dve.wait_ge(prep.pool.sem, prep.pool.after(n, "xg"))
                dve.wait_ge(kept, n)
                nc.vector.tensor_tensor(x1[:], xb(n), xt[:], ALU.add).then_inc(post_dve.sem, 1)
                dve.wait_ge(post_dve.sem, post_dve.after(n, "x1"))
                for i in range(I):
                    nc.vector.bn_stats(bst2[:, i, :], x1[:, i, :]).then_inc(post_dve.sem, 1)
                dve.wait_ge(post_dve.sem, post_dve.after(n, "bn1"))
                nc.vector.tensor_copy(bst[:, ds(n * I, I), :], bst2[:]).then_inc(post_dve.sem, 1)

            def iteration(n, par, first=False, makes=True, ahead=True):
                if makes:
                    norm_qk(n + 1, prep)
                    split_q(n + 1, prep)
                if not first:
                    normalise(n - 1)
                if ahead:
                    stack(n + 2, prep)
                if makes:
                    k_out(n + 1, prep, 1 - par)
                    q_out(n + 1, prep)
                    widen(n + 1, prep, 1 - par)
                if not first:
                    channels(n - 1)
                if ahead:
                    xT_out(n + 2, prep)
                if not first:
                    projected(n - 1)
                    residual(n - 1)

            iteration(0, 0, first=True)
            with dve.Fori(0, (B - 4) // 2) as it:
                iteration(it * 2 + 1, 1)
                iteration(it * 2 + 2, 0)
            iteration(B - 3, 1)
            iteration(B - 2, 0, ahead=False)
            iteration(B - 1, 1, makes=False, ahead=False)
            normalise(B - 1)
            channels(B - 1)
            projected(B - 1)
            residual(B - 1)

            def norm2(k):
                L = ln2_dve

                def made(name, k=k):
                    dve.wait_ge(L.sem, L.after(k, name))

                xk = xall[:, 2 * k:2 * k + 2, :].rearrange("p b (i c) -> p (b i) c", i=I)
                for t in range(T):
                    nc.vector.tensor_scalar(z2[:, t, :], xk[:, t, :], mv2[:, T * k + t, 0:1],
                                            rstd2[:, T * k + t:T * k + t + 1],
                                            ALU.subtract, ALU.mult).then_inc(L.sem, 1)
                made("z3")

                def m2(r):
                    return mbc[:, 2 * k:2 * k + 2, r * H:(r + 1) * H].unsqueeze(2).broadcast_to([P, 2, I, H])

                def by_batch(t):
                    return t.rearrange("p (b i) c -> p b i c", i=I)

                nc.vector.tensor_tensor(by_batch(z2a), by_batch(z2), m2(A2), ALU.mult).then_inc(L.sem, 1)
                made("za")
                nc.vector.tensor_tensor(by_batch(z2m), by_batch(z2a), m2(B2), ALU.add).then_inc(L.sem, 1)
                made("zm")
                if k:
                    dve.wait_ge(ln2_pe.sem, ln2_pe.after(k - 1, "zT1"))
                zc = z2m.rearrange("p t (c w) -> p (t c) w", w=CW)
                slots = zst[:, :, 0:3 * CW].rearrange("p t (s w) -> p t s w", w=CW)
                nc.vector.tensor_copy(slots[:, :, 0:3:2, :], zc.unsqueeze(2).broadcast_to([P, T * NC, 2, CW])
                                      ).then_inc(L.sem, 1)
                made("zhi")
                nc.vector.tensor_tensor(slots[:, :, 1, :], zc, slots[:, :, 0, :], ALU.subtract).then_inc(L.sem, 1)
                for h in range(2):
                    dve.wait_ge(ln2_pe.sem, ln2_pe.after(k, f"zT{h}"))
                    if k >= 2:
                        dve.wait_ge(hid_pe, NF * (k - 1))
                    nc.vector.tensor_copy(zT[k % 2][:, 2 * h:2 * h + 2, :], bank16(h, 2)[0:KR]).then_inc(L.sem, 1)

            dve.wait_ge(post_dve.sem, post_dve.after(B - 1, "bs"))
            for t in range(B * I):
                nc.vector.bn_aggr(mv2[:, t, :], bst[:, t, :]).then_inc(stat2, 1)
            dve.wait_ge(kept, B)
            dve.wait_ge(root_act.sem, root_act.after(0, "y0"))
            newton(nc, dve, root_dve, 0, nt2, y2, mv2[:, :, 1], rstd2)
            dve.wait_ge(root_dve.sem, root_dve.after(0, "rstd"))
            norm2(0)
            for k in range(NB):
                if k + 1 < NB:
                    norm2(k + 1)
                dve.wait_ge(res_pool, k + 1)
                for n in range(2):
                    dve.wait_ge(y_pe, 2 * k + n + 1)
                    if k:
                        dve.wait_ge(fin_dve.sem, fin_dve.after(k - 1, f"yo{n}"))
                    b = 2 * k + n
                    nc.vector.tensor_tensor(yg[:, n, :].rearrange("p (i c) -> p i c", i=I),
                                            ps_o[:, n, 0:I * H].rearrange("p (i c) -> p i c", i=I), mb(b, GM),
                                            ALU.mult).then_inc(fin_dve.sem, 1)
                    dve.wait_ge(fin_dve.sem, fin_dve.after(k, f"yg{n}"))
                    if k >= 2:
                        dve.wait_ge(stored[k % 2], 16 * (k // 2))
                    nc.vector.tensor_tensor(yo[k % 2][:, n, :], yg[:, n, :], xall[:, b, :], ALU.add
                                            ).then_inc(fin_dve.sem, 1)

        @block.tensor
        def _(pe):
            pe.wait_ge(ld_wm, 16)
            pe.wait_ge(set_dve.sem, set_dve.after(0, "c_s"))
            for a in range(2):
                for h in range(2):
                    mm = nc.tensor.matmul(ps_s[0:B, a, 0:3 * H], c_s[:, h, :], wm_sb[:, h, a * 3 * H:(a + 1) * 3 * H],
                                          start=(h == 0), stop=(h == 1))
            mm.then_inc(set_pe, 1)
            pe.wait_ge(set_dve.sem, set_dve.after(0, "wq"))

            def transpose_x(b, S):
                pe.wait_ge(S.x.sem, S.x.after(b, "xlo"))
                for c in range(NC):
                    for i in range(I):
                        tr = nc.tensor.transpose(bank16(1)[0:KR, c, i * P:(i + 1) * P], xst[:, i * NC + c, 0:KR], id16[:])
                tr.then_inc(S.pe.sem, 1)

            def make_qkv(b, S):
                pe.wait_ge(S.x.sem, S.x.after(b, "xT"))
                for i in range(I):
                    for c in range(NC):
                        mm = nc.tensor.matmul(ps_x[:, i, 0:QKV], xT[:, c, i * P:(i + 1) * P], wq[:, c, :],
                                              start=(c == 0), stop=(c == NC - 1))
                mm.then_inc(S.pe.sem, 1)

            def transpose_heads(b, S, st, bank):
                for j in range(JG):
                    for i in range(I):
                        tr = nc.tensor.transpose(bank16(bank)[:, j, i * P:(i + 1) * P],
                                                 st[:, i * NH + 4 * j:i * NH + 4 * j + 4, :].rearrange("p h s -> p (h s)"),
                                                 id16[:])
                tr.then_inc(S.pe.sem, 1)

            def qkv_used(b, S):
                pe.wait_ge(S.act.sem, S.act.after(b, "v"))
                pe.wait_ge(S.dve.sem, S.dve.after(b, "qn"))

            def transpose_k(b, S):
                pe.wait_ge(S.dve.sem, S.dve.after(b, "klo"))
                transpose_heads(b, S, kst, 0)

            def transpose_q(b, S):
                pe.wait_ge(S.dve.sem, S.dve.after(b, "qlo"))
                pe.wait_ge(S.gain.sem, S.gain.after(b, "sh"))
                transpose_heads(b, S, qst, 1)

            with pe.If(needs_max(pe) == 1):
                with pe.Fori(0, B) as b:
                    pe.wait_ge(gen_dve.sem, gen_dve.after(b - 1, "lo"))
                    transpose_x(b, pre)
                    make_qkv(b, pre)
                    qkv_used(b, pre)
                    transpose_k(b, pre)
                    transpose_q(b, pre)
                    pe.wait_ge(pre.dve.sem, pre.dve.after(b, "kT"))
                    pe.wait_ge(pre.wide.sem, pre.wide.after(b, "g3"))
                    for m in range(I * NH // 2):
                        if m >= 2:
                            pe.wait_ge(gen_max, b * (I * NH // 2) + (m - 1))
                        i, h = divmod(2 * m, NH)
                        for g in range(2):
                            j, r = divmod(h + g, 4)
                            mm = nc.tensor.matmul(ps_x[:, m % 2, g * N:(g + 1) * N], qT[0][:, j, r, i * P:(i + 1) * P],
                                                  kT[0][:, j, :], start=True, stop=True)
                        mm.then_inc(gen_pe, 1)
                pe.wait_ge(gen_dve.sem, gen_dve.after(B - 1, "lo"))

            transpose_x(0, prep)
            make_qkv(0, prep)
            qkv_used(0, prep)
            transpose_k(0, prep)
            transpose_q(0, prep)
            pe.wait_ge(prep.dve.sem, prep.dve.after(0, "qT"))
            transpose_x(1, prep)

            def scores(n, u, par):
                j, i = divmod(u, 2)
                if u == 0:
                    pe.wait_ge(prep.dve.sem, prep.dve.after(n, "kT"))
                    pe.wait_ge(prep.wide.sem, prep.wide.after(n, "g3"))
                if is_later(n) or u >= 2:
                    pe.wait_ge(exped, n * U + (u - 1))
                for a in range(2):
                    mm = nc.tensor.matmul(ps_s[:, 2 * (u % 2) + a, :], kT[par][:, j, i * P:(i + 1) * P],
                                          qT[par][:, j, 2 * a:2 * a + 2, :], start=True, stop=True)
                mm.then_inc(scored, 1)

            def values(n, u, par):
                j, i = divmod(u, 2)
                pe.wait_ge(exped, n * U + (u + 1))
                if i == 0 and (is_later(n) or j >= 2):
                    pe.wait_ge(o_out, n * JG + (j - 1))
                for g in range(4):
                    mm = nc.tensor.matmul(ps_o[SLOT * g:SLOT * (g + 1), j % 2, 0:N], v[par][:, i, 4 * j + g, :],
                                          pT[u % NP][:, g, :], start=(i == 0), stop=(i == I - 1))
                mm.then_inc(summed, 1)

            def transpose_o(n, par):
                pe.wait_ge(o_out, (n + 1) * JG)
                for i in range(I):
                    for j in range(JG):
                        tr = nc.tensor.transpose(ps_x[:, i, j * P:(j + 1) * P], oT[par][:, j, i * P:(i + 1) * P], id32[:])
                tr.then_inc(post_pe.sem, 1)

            def transpose_o_tok(n):
                pe.wait_ge(post_dve.sem, post_dve.after(n, "o"))
                ov = o_tok[:].rearrange("p (i h) d -> p i (h d)", i=I)
                for c in range(2):
                    for i in range(I):
                        tr = nc.tensor.transpose(ps_x[0:HT, 0, c * N + i * P:c * N + (i + 1) * P],
                                                 ov[:, i, c * HT:(c + 1) * HT], id32[:])
                tr.then_inc(post_pe.sem, 1)

            def project(n):
                pe.wait_ge(post_dve.sem, post_dve.after(n, "och"))
                for i in range(I):
                    for c in range(2):
                        mm = nc.tensor.matmul(ps_x[:, 0, i * H:(i + 1) * H], o_ch[:, c, i * P:(i + 1) * P], wp_sb[:, c, :],
                                              start=(c == 0), stop=(c == 1))
                mm.then_inc(post_pe.sem, 1)

            def iteration(n, par, first=False, makes=True, ahead=True):
                if not first:
                    values(n - 1, 7, 1 - par)
                scores(n, 1, par)
                if makes:
                    if not first:
                        pe.wait_ge(gated, n - 1)
                    make_qkv(n + 1, prep)
                for u in range(3):
                    values(n, u, par)
                    scores(n, u + 2, par)
                if makes:
                    qkv_used(n + 1, prep)
                else:
                    pe.wait_ge(gated, n - 1)
                if not first:
                    transpose_o(n - 1, 1 - par)
                values(n, 3, par)
                scores(n, 5, par)
                scores(n, 6, par)
                if not first:
                    pe.wait_ge(post_dve.sem, post_dve.after(n - 1, "o"))
                if makes:
                    transpose_k(n + 1, prep)
                    transpose_q(n + 1, prep)
                values(n, 4, par)
                scores(n, 7, par)
                if makes:
                    pe.wait_ge(prep.dve.sem, prep.dve.after(n + 1, "kT"))
                if not first:
                    transpose_o_tok(n - 1)
                values(n, 5, par)
                if ahead:
                    pe.wait_ge(prep.dve.sem, prep.dve.after(n + 1, "qT"))
                    transpose_x(n + 2, prep)
                values(n, 6, par)
                if makes:
                    scores(n + 1, 0, 1 - par)
                if not first:
                    project(n - 1)

            pe.wait_ge(ld_w, 32)
            scores(0, 0, 0)
            iteration(0, 0, first=True)
            with pe.Fori(0, (B - 4) // 2) as it:
                iteration(it * 2 + 1, 1)
                iteration(it * 2 + 2, 0)
            iteration(B - 3, 1)
            iteration(B - 2, 0, ahead=False)
            iteration(B - 1, 1, makes=False, ahead=False)
            values(B - 1, 7, 1)
            pe.wait_ge(gated, B - 1)
            transpose_o(B - 1, 1)
            transpose_o_tok(B - 1)
            project(B - 1)

            def transpose_z(k):
                pe.wait_ge(ln2_dve.sem, ln2_dve.after(k, "zlo"))
                if k == 0:
                    pe.wait_ge(gated, B)
                for h in range(2):
                    if k:
                        pe.wait_ge(ln2_dve.sem, ln2_dve.after(k - 1, f"zT{h}"))
                    for c in range(2):
                        for t in range(T):
                            tr = nc.tensor.transpose(bank16(h, 2)[0:KR, c, t * P:(t + 1) * P],
                                                     zst[:, t * NC + 2 * h + c, 0:KR], id16[:])
                    tr.then_inc(ln2_pe.sem, 1)

            transpose_z(0)
            pe.wait_ge(w1_made, 3)
            for k in range(NB):
                pe.wait_ge(ln2_dve.sem, ln2_dve.after(k, "zT1"))
                for f in range(NF):
                    m = NF * k + f
                    if m >= 4:
                        pe.wait_ge(gelued, m - 3)
                    for c in range(NC):
                        mm = nc.tensor.matmul(ps_s[0:FW[f], m % 4, :], w1s[:, c, f * FT:f * FT + FW[f]], zT[k % 2][:, c, :],
                                              start=(c == 0), stop=(c == NC - 1))
                    mm.then_inc(hid_pe, 1)
                if k + 1 < NB:
                    transpose_z(k + 1)
                pe.wait_ge(gelued, NF * (k + 1))
                for n in range(2):
                    if k:
                        pe.wait_ge(fin_dve.sem, fin_dve.after(k - 1, f"yg{n}"))
                    for i in range(I):
                        t = n * I + i
                        for f in range(NF):
                            mm = nc.tensor.matmul(ps_o[:, n, i * H:(i + 1) * H], hT[k % 2][0:FW[f], f, t * P:(t + 1) * P],
                                                  w2_sb[0:FW[f], f, :], start=(f == 0), stop=(f == NF - 1))
                    mm.then_inc(y_pe, 1)


def newton(nc, dve, steps, b, t, y, var, result):
    nc.vector.scalar_tensor_tensor(t[:], y[:], HALF_STEP, y[:], ALU.mult, ALU.mult).then_inc(steps.sem, 1)
    dve.wait_ge(steps.sem, steps.after(b, "n1"))
    nc.vector.scalar_tensor_tensor(t[:], var, EPS, t[:], ALU.add, ALU.mult).then_inc(steps.sem, 1)
    dve.wait_ge(steps.sem, steps.after(b, "n2"))
    nc.vector.scalar_tensor_tensor(result[:], t[:], 1.5, y[:], ALU.add, ALU.mult).then_inc(steps.sem, 1)


def kernel(**inputs):
    import numpy as np
    import concourse.bacc as bacc
    from concourse.bass_utils import run_bass_kernel_spmd

    def f(name):
        return np.ascontiguousarray(np.asarray(inputs[name]))

    def stacked(w, bias):
        n = w.shape[1]
        a = np.zeros((KR, NC, n), w.dtype)
        for s in range(3):
            a[s * CW:(s + 1) * CW] = w.reshape(NC, CW, n).transpose(1, 0, 2)
        a[3 * CW:, 0] = bias
        return a

    def halves(w):
        return np.ascontiguousarray(w.reshape(2, HT, -1).transpose(1, 0, 2))

    w2 = f("L0_cond_w2")
    w2p = np.zeros((NF * FT, H), w2.dtype)
    w2p[:MLP] = w2
    lo_rows = np.zeros((KR, 1), np.float32)
    lo_rows[2 * CW:3 * CW] = 1.0
    lo_rows[KR - 1] = 1.0
    arrays = {
        "x": f("x"),
        "cT": halves(f("cond_1152").T),
        "w_mod": halves(f("L0_cond_w_mod")),
        "b_mod": f("L0_cond_b_mod"),
        "w_qkv": stacked(f("L0_cond_w_qkv"), f("L0_cond_b_qkv")),
        "g_q": f("L0_cond_g_q"),
        "g_k": f("L0_cond_g_k"),
        "w_proj": halves(f("L0_cond_w_proj")),
        "b_proj": f("L0_cond_b_proj"),
        "w1": stacked(f("L0_cond_w1"), f("L0_cond_b1")),
        "w2": np.ascontiguousarray(w2p.reshape(NF, FT, H).transpose(1, 0, 2)),
        "b2": f("L0_cond_b2"),
        "ident": np.eye(P, dtype=np.float32),
        "lo_rows": lo_rows,
    }
    nc = bacc.Bacc("TRN2", target_bir_lowering=False, num_devices=1)
    args = [nc.dram_tensor("in_" + n, a.shape, mybir.dt.from_np(a.dtype), kind="ExternalInput").ap()
            for n, a in arrays.items()]
    out = nc.dram_tensor("out", (B, N, H), F32, kind="ExternalOutput").ap()
    build(nc, *args, out)
    r = run_bass_kernel_spmd(nc, [{"in_" + n: a for n, a in arrays.items()}], core_ids=[0])
    return r.results[0]["out"]
```

```python
from contextlib import ExitStack

import concourse.bass as bass
from concourse import mybir

F32 = mybir.dt.float32
F16 = mybir.dt.float16
I32 = mybir.dt.int32
ACT = mybir.ActivationFunctionType
ALU = mybir.AluOpType
AX = mybir.AxisListType
ds = bass.ds

B, N, H = 8, 256, 144
NH, HD = 16, 9
MLP = 4 * H
P = 128
I = N // P
QKV = 3 * H
EPS = 1e-6
JG = 4
SLOT = 32
NC = 4
CW = H // NC
KR = 3 * CW + 2
HT = H // 2
FT = 120
NF = 5
FW = [FT, FT, FT, FT, MLP - 4 * FT]
U = 8
XS, WS = 2.0 ** 4, 2.0 ** 8
QS = 2.0 ** 12
UNSCALE = 1.0 / (XS * WS)
SAFE_BOUND = 60.0
HALF_STEP = -0.5
MODS = 8
A1, A2, B1, B2, GA, GM, GAB, GMB = range(MODS)


class Steps:

    def __init__(self, sem, names):
        self.sem, self.names = sem, names.split()

    def after(self, b, name):
        return b * len(self.names) + (self.names.index(name) + 1)


class Prep:

    def __init__(self, sem, tag):
        self.pool = Steps(sem(tag + "_pool"), "z0 z1 za xm")
        self.gain = Steps(sem(tag + "_gain"), "sh qg")
        self.dve = Steps(sem(tag + "_dve"), "ssum n1 n2 rstd kn qn khi klo qhi qlo kT qT")
        self.wide = Steps(sem(tag + "_wide"), "g0 g1 g2 g3 g4 g5 g6 g7")
        self.x = Steps(sem(tag + "_x"), "xhi xlo xT")
        self.act = Steps(sem(tag + "_act"), "sq raw ln y0")
        self.pe = Steps(sem(tag + "_pe"), "kT qT")
        self.qkv = Steps(sem(tag + "_qkv"), "qkv")
        self.xpe = Steps(sem(tag + "_xpe"), "xT")


class Stats:

    def __init__(self, sem, tag, tiles):
        self.tiles = tiles
        self.of = slice(tiles.start, tiles.stop)
        self.bn = sem(tag + "_bn")
        self.act = Steps(sem(tag + "_ln"), "ln y0")
        self.root = Steps(sem(tag + "_root"), "n1 n2 rstd")


def build(nc, x, cT, w_mod, b_mod, w_qkv, g_q, g_k, w_proj, b_proj, w1, w2, b2, ident, lo_rows, out):
    with ExitStack() as ctx:
        def sb(name, shape, dt=F32):
            return ctx.enter_context(nc.sbuf_tensor(name, shape, dt))

        def sem(name):
            return ctx.enter_context(nc.semaphore(name))

        id32 = sb("id32", [P, P])
        id16 = sb("id16", [P, P], F16)
        lo_row = sb("lo_row", [KR, 1])
        eps = sb("eps", [P, 1])
        c_sb = sb("c_sb", [HT, 2, B])
        c_e = sb("c_e", [HT, 2, B])
        c_s = sb("c_s", [HT, 2, B])
        bm_sb = sb("bm_sb", [B, 6 * H])
        bias2 = sb("bias2", [B, 2, H])
        mod = sb("mod", [B, 6 * H])
        mrow = sb("mrow", [B, MODS, H])
        mbc = sb("mbc", [P, B, MODS * H])
        gqk = sb("gqk", [P, 2, HD])
        gp = sb("gp", [P, HD])
        gneg = sb("gneg", [P, HD])
        gabs = sb("gabs", [P, HD])
        gmax = sb("gmax", [P, 1])
        gsafe = sb("gsafe", [P, 1])
        ginv = sb("ginv", [P, 1])
        gbc = sb("gbc", [P, NH, HD])
        escale = sb("escale", [P, 1])
        flagf = sb("flagf", [P, 1])
        flag = sb("flag", [P, 1], I32)
        wq_m = sb("wq_m", [KR, NC, 2 * NH])
        wq_h = sb("wq_h", [KR, NC, QKV], F16)
        wq = sb("wq", [KR, NC, QKV], F16)
        w1s = sb("w1s", [KR, NC, MLP], F16)
        w2_sb = sb("w2_sb", [FT, NF, H])
        wp_sb = sb("wp_sb", [HT, 2, H])

        xall = sb("xall", [P, B, I * H])
        bst = sb("bst", [P, B * I, 6])
        mv = sb("mv", [P, B * I, 2])
        ly = sb("ly", [P, B * I])
        y0 = sb("y0", [P, B * I])
        nt = sb("nt", [P, B * I])
        rstd = sb("rstd", [P, B * I])
        z = sb("z", [P, I, H])
        xa = sb("xa", [P, I, H])
        xm = sb("xm", [P, I, H])
        xst = sb("xst", [P, I * NC, P], F16)
        xT = sb("xT", [KR, NC, N], F16)
        sq = sb("sq", [P, I, 2 * H])
        ssum = sb("ssum", [P, I * 2 * NH])
        qly = sb("qly", [P, I * 2 * NH])
        qy0 = sb("qy0", [P, I * 2 * NH])
        qnt = sb("qnt", [P, I * 2 * NH])
        qrs = sb("qrs", [P, I * 2 * NH])
        raw = sb("raw", [P, I, QKV])
        qn = sb("qn", [P, I, H])
        kn = sb("kn", [P, I, H])
        qg = sb("qg", [P, I, H])
        qst = sb("qst", [P, I * NH, SLOT], F16)
        kst = sb("kst", [P, I * NH, SLOT], F16)
        v = [sb(f"v{i}", [P, I, NH, SLOT]) for i in range(2)]
        qP = sb("qP", [P, JG, N], F16)
        kT = [sb(f"kT{i}", [P, JG, N], F16) for i in range(2)]
        qT = [sb(f"qT{i}", [P, JG, 4, N], F16) for i in range(2)]
        shift = sb("shift", [P, B, I * NH * 3], F16)
        rmax = sb("rmax", [P, I * NH])
        sres = sb("sres", [P, I * NH])
        NP = 4
        pTs = sb("pTs", [P, NP, 4 * N])
        pT = [pTs[:, i, :].rearrange("p (g n) -> p g n", g=4) for i in range(NP)]
        wm_sb = pTs[0:HT].rearrange("p i n -> p (i n)")[:, 0:12 * H].rearrange("p (h n) -> p h n", h=2)
        oT = [sb(f"oT{i}", [P, JG, N]) for i in range(2)]
        rden = sb("rden", [P, I * NH])
        o_tok = sb("o_tok", [P, I * NH, HD])
        o_ch = sb("o_ch", [HT, 2, N])
        xt = sb("xt", [P, I, H])

        NB = B // 2
        T = 2 * I
        EARLY = (NB - 1) * T
        bst2 = sb("bst2", [P, I, 6])
        x1 = sb("x1", [P, I, H])
        mv2 = sb("mv2", [P, B * I, 2])
        ly2 = sb("ly2", [P, B * I])
        y2 = sb("y2", [P, B * I])
        nt2 = sb("nt2", [P, B * I])
        minus_half = sb("minus_half", [P, T])
        rstd2 = sb("rstd2", [P, B * I])
        z2s = sb("z2s", [P, 3, T, H])
        z2, z2a, z2m = (z2s[:, i] for i in range(3))
        wq_f = z2s[0:KR].rearrange("p a t c -> p (a t c)").rearrange("p (c n) -> p c n", c=NC)
        zst = sb("zst", [P, T * NC, P], F16)
        late = sb("late", [P, B * MODS * H])
        mflat = late[0:1, :].rearrange("p (b m) -> p b m", b=B)
        at = 0
        hT, zT, yo = [], [], []
        for i in range(2):
            hT.append(late[0:FT, at:at + NF * T * P].rearrange("p (f n) -> p f n", f=NF))
            at += NF * T * P
            zT.append(late[0:KR, at:at + NC * T * P // 2].bitcast(F16).rearrange("p (c n) -> p c n", c=NC))
            at += NC * T * P // 2
            yo.append(late[:, at:at + T * H].rearrange("p (b n) -> p b n", b=2))
            at += T * H
        yg = late[:, at:at + T * H].rearrange("p (b n) -> p b n", b=2)
        at += T * H
        w1_f = late[0:KR, at // 2:at // 2 + NC * MLP].rearrange("p (c n) -> p c n", c=NC)
        w1_h = late[0:KR, at - NC * MLP // 2:at].bitcast(F16).rearrange("p (c n) -> p c n", c=NC)

        ps_s = ctx.enter_context(nc.psum_tensor("ps_s", [P, 4, 512], F32))
        ps_o = ctx.enter_context(nc.psum_tensor("ps_o", [P, 2, 512], F32))
        ps_x = ctx.enter_context(nc.psum_tensor("ps_x", [P, 2, 512], F32))

        def bank16(i, c=4):
            return ps_x[:, i, :].bitcast(F16).rearrange("p (c n) -> p c n", c=c)

        first_o = ps_o[:, 0, :].bitcast(F16).rearrange("p (c n) -> p c n", c=NC)

        ld_c, ld_wm, ld_x, ld_wq, ld_id, ld_g, ld_w, ld_w1, ld_b = (
            sem(s) for s in "ld_c ld_wm ld_x ld_wq ld_id ld_g ld_w ld_w1 ld_b".split())
        ld_flat = sem("ld_flat")
        zeroed = sem("zeroed")
        ones_set = sem("ones_set")
        mod_bc = sem("mod_bc")
        w1_made = sem("w1_made")
        set_dve = Steps(sem("set_dve"), "eps c1 c2 c_s gp gneg gabs gmax gsafe ginv gbc escale flagf flag "
                        "id16 mod mA mB mG mGB mean centred wq_h wq")
        first_stats = Stats(sem, "first_stats", range(2 * I))
        rest_stats = Stats(sem, "rest_stats", range(2 * I, B * I))
        gen_stats = Stats(sem, "gen_stats", range(2 * I, B * I))
        set_act = Steps(sem("set_act"), "c_e")
        set_pe = sem("set_pe")
        pre = Prep(sem, "pre")
        gen_pe = sem("gen_pe")
        gen_max = sem("gen_max")
        gen_dve = Steps(sem("gen_dve"), "s0 hi r1 mid r2 lo")
        gen_bc = sem("gen_bc")
        prep = Prep(sem, "prep")
        v_in = sem("v_in")
        biased = sem("biased")
        scored = sem("scored")
        exped = sem("exped")
        summed = sem("summed")
        o_out = sem("o_out")
        post_pe = Steps(sem("post_pe"), "otok och proj")
        post_dve = Steps(sem("post_dve"), "rden o och x1 bn0 bn1 bs")
        gated = sem("gated")
        kept = sem("kept")
        ln2_z = Steps(sem("ln2_z"), "z0 z1 z2 z3")
        ln2_mod = Steps(sem("ln2_mod"), "za zm")
        ln2_parts = Steps(sem("ln2_parts"), "zhi zlo")
        ln2_T = Steps(sem("ln2_T"), "zT0 zT1")
        stat2 = sem("stat2")
        root_dve = Steps(sem("root_dve"), "n1 n2 rstd")
        root_act = Steps(sem("root_act"), "ln y0")
        root_pool = sem("root_pool")
        ln2_pe = Steps(sem("ln2_pe"), "zT0 zT1")
        res_pool = sem("res_pool")
        hid_pe = sem("hid_pe")
        gelued = sem("gelued")
        y_pe = sem("y_pe")
        fin_dve = Steps(sem("fin_dve"), "yg0 yo0 yg1 yo1")
        stored = [sem(f"stored{i}") for i in range(2)]

        block = ctx.enter_context(nc.Block())

        def xb(b):
            return xall[:, ds(b, 1), :].rearrange("p o (i c) -> p (o i) c", i=I)

        def mb(b, k):
            return mbc[:, ds(b, 1), k * H:(k + 1) * H].broadcast_to([P, I, H])

        def is_later(b, S=prep):
            return S is prep and (not isinstance(b, int) or b > 0)

        def two_before(b):
            return not isinstance(b, int) or b > 1

        def needs_max(eng):
            eng.wait_ge(set_dve.sem, set_dve.after(0, "flag"))
            return eng.value_load(flag[0:1, 0:1], min_val=0, max_val=1)

        @block.sync
        def _(sp):
            sp.dma_start(c_sb[:], cT).then_inc(ld_c, 16)
            sp.dma_start(wm_sb, w_mod).then_inc(ld_wm, 16)
            sp.dma_start(xall[:], x.rearrange("b (p i) c -> p b (i c)", i=I)).then_inc(ld_x, 16)
            sp.dma_start(wq_f, w_qkv).then_inc(ld_wq, 16)
            sp.dma_start(lo_row[:], lo_rows).then_inc(ld_wq, 16)
            sp.dma_start(id32[:], ident).then_inc(ld_id, 16)
            sp.dma_start(w2_sb[:], w2).then_inc(ld_w, 16)
            sp.dma_start(wp_sb[:], w_proj).then_inc(ld_w, 16)
            sp.wait_ge(set_dve.sem, set_dve.after(0, "mGB"))
            sp.dma_start(mflat, mrow[:].rearrange("b m h -> b (m h)")).then_inc(ld_flat, 16)
            sp.wait_ge(mod_bc, B)
            sp.dma_start(w1_f, w1).then_inc(ld_w1, 16)
            for k in range(NB - 1):
                sp.wait_ge(fin_dve.sem, fin_dve.after(k, "yo1"))
                sp.dma_start(out[2 * k:2 * k + 2].rearrange("b (p i) c -> p b (i c)", i=I),
                             yo[k % 2]).then_inc(stored[k % 2], 16)
            for n in range(2):
                sp.wait_ge(fin_dve.sem, fin_dve.after(NB - 1, f"yo{n}"))
                sp.dma_start(out[B - 2 + n].rearrange("(p i) c -> p (i c)", i=I),
                             yo[(NB - 1) % 2][:, n, :]).then_inc(stored[(NB - 1) % 2], 16)
            sp.wait_ge(stored[0], 16 * (NB // 2))
            sp.wait_ge(stored[1], 16 * (NB // 2 + 1))

        @block.gpsimd
        def _(pool):
            for t in (xst, qst, kst, zst, shift):
                nc.gpsimd.memset(t[:].bitcast(F32), 0.0).then_inc(zeroed, 1)
            for i in range(2):
                nc.gpsimd.memset(v[i][:], 0.0).then_inc(zeroed, 1)
                nc.gpsimd.memset(qT[i][:].bitcast(F32), 0.0).then_inc(zeroed, 1)
            pool.wait_ge(zeroed, 9)
            nc.gpsimd.memset(minus_half[:], -0.5).then_inc(ones_set, 1)
            nc.gpsimd.memset(xst[:, :, 3 * CW:KR], XS).then_inc(ones_set, 1)
            nc.gpsimd.memset(zst[:, :, 3 * CW:KR], XS).then_inc(ones_set, 1)
            nc.gpsimd.memset(kst[:, :, 3 * HD:3 * HD + 3], QS).then_inc(ones_set, 1)
            for i in range(2):
                nc.gpsimd.memset(v[i][:, :, :, HD:HD + 1], 1.0 / UNSCALE).then_inc(ones_set, 1)

            def spread(b, done=mod_bc):
                nc.gpsimd.partition_broadcast(mbc[:, b, :], mflat[:, b, :], P).then_inc(done, 1)

            def standardise(b, S):
                if is_later(b, S):
                    pool.wait_ge(S.pool.sem, S.pool.after(b - 1, "za"))
                nc.gpsimd.tensor_tensor(z[:], xb(b), mv[:, ds(b * I, I), 0:1].broadcast_to([P, I, H]),
                                        ALU.subtract).then_inc(S.pool.sem, 1)
                pool.wait_ge(S.pool.sem, S.pool.after(b, "z0"))
                nc.gpsimd.tensor_tensor(z[:], z[:], rstd[:, ds(b * I, I)].unsqueeze(2).broadcast_to([P, I, H]),
                                        ALU.mult).then_inc(S.pool.sem, 1)

            def modulate(b, S):
                if isinstance(b, int):
                    pool.wait_ge(mod_bc, b + 1)
                if is_later(b, S):
                    pool.wait_ge(S.pool.sem, S.pool.after(b - 1, "xm"))
                pool.wait_ge(S.pool.sem, S.pool.after(b, "z1"))
                nc.gpsimd.tensor_tensor(xa[:], z[:], mb(b, A1), ALU.mult).then_inc(S.pool.sem, 1)
                pool.wait_ge(S.pool.sem, S.pool.after(b, "za"))
                if is_later(b, S):
                    pool.wait_ge(S.x.sem, S.x.after(b - 1, "xlo"))
                nc.gpsimd.tensor_tensor(xm[:], xa[:], mb(b, B1), ALU.add).then_inc(S.pool.sem, 1)

            def bias_in(b):
                nc.gpsimd.tensor_tensor(xb(b), xb(b), mb(b, GAB), ALU.add).then_inc(biased, 1)

            def gains(b, S):
                if is_later(b, S):
                    pool.wait_ge(S.pe.sem, S.pe.after(b - 1, "qT"))
                nc.gpsimd.tensor_copy(qst[:, :, 3 * HD:3 * HD + 3],
                                      shift[:, ds(b, 1), :].rearrange("p o (t s) -> p (o t) s", s=3)
                                      ).then_inc(S.gain.sem, 1)
                pool.wait_ge(S.dve.sem, S.dve.after(b, "qn"))
                if is_later(b, S):
                    pool.wait_ge(S.dve.sem, S.dve.after(b - 1, "qlo"))
                nc.gpsimd.tensor_tensor(qg[:], qn[:], gbc[:].rearrange("p (o h) d -> p o (h d)", o=1)
                                        .broadcast_to([P, I, H]), ALU.mult).then_inc(S.gain.sem, 1)

            def v_slots(b, par):
                pool.wait_ge(prep.act.sem, prep.act.after(b, "raw"))
                if two_before(b):
                    pool.wait_ge(summed, (b - 1) * U)
                nc.gpsimd.tensor_copy(v[par][:, :, :, 0:HD],
                                      raw[:, :, 2 * H:3 * H].rearrange("p i (h d) -> p i h d", d=HD)).then_inc(v_in, 1)

            with pool.If(needs_max(pool) == 1):
                pool.wait_ge(first_stats.root.sem, first_stats.root.after(0, "rstd"))
                pool.wait_ge(gen_stats.root.sem, gen_stats.root.after(0, "rstd"))
                pool.wait_ge(ld_flat, 16)
                for b in range(B):
                    spread(b, gen_bc)
                pool.wait_ge(gen_bc, B)
                with pool.Fori(0, B) as b:
                    pool.wait_ge(gen_dve.sem, gen_dve.after(b - 1, "lo"))
                    standardise(b, pre)
                    modulate(b, pre)
                    gains(b, pre)
                pool.wait_ge(gen_dve.sem, gen_dve.after(B - 1, "lo"))

            pool.wait_ge(ld_flat, 16)
            spread(0)
            pool.wait_ge(first_stats.root.sem, first_stats.root.after(0, "rstd"))
            standardise(0, prep)
            modulate(0, prep)
            spread(1)
            standardise(1, prep)
            modulate(1, prep)
            spread(2)
            pool.wait_ge(ones_set, 6)
            v_slots(0, 0)
            gains(0, prep)
            bias_in(0)
            bias_in(1)
            pool.wait_ge(rest_stats.root.sem, rest_stats.root.after(0, "rstd"))
            standardise(2, prep)
            modulate(2, prep)
            bias_in(2)

            def keep(n):
                pool.wait_ge(post_dve.sem, post_dve.after(n, "x1"))
                nc.gpsimd.tensor_copy(xb(n), x1[:]).then_inc(kept, 1)

            def iteration(n, par, keeps=True, norms=True):
                v_slots(n + 1, 1 - par)
                gains(n + 1, prep)
                if norms:
                    standardise(n + 3, prep)
                    modulate(n + 3, prep)
                    bias_in(n + 3)
                if keeps:
                    keep(n - 2)

            spread(3)
            iteration(0, 0, keeps=False)
            for b in range(4, B):
                spread(b)
            pool.wait_ge(mod_bc, B)
            iteration(1, 1, keeps=False)
            with pool.Fori(1, 2) as it:
                iteration(it * 2, 0)
                iteration(it * 2 + 1, 1)
            iteration(B - 4, 0)
            iteration(B - 3, 1, norms=False)
            iteration(B - 2, 0, norms=False)
            pool.wait_ge(ld_w1, 16)
            nc.gpsimd.tensor_scalar(w1_h, w1_f, WS, lo_row[:, 0:1], ALU.mult, ALU.mult).then_inc(w1_made, 1)
            keep(B - 3)

            def by_batch(t):
                return t.rearrange("p (b i) c -> p b i c", i=I)

            def m2(k, r):
                return mbc[:, 2 * k:2 * k + 2, r * H:(r + 1) * H].unsqueeze(2).broadcast_to([P, 2, I, H])

            def modulate2(k):
                pool.wait_ge(ln2_z.sem, ln2_z.after(k, "z3"))
                if k:
                    pool.wait_ge(ln2_mod.sem, ln2_mod.after(k - 1, "zm"))
                nc.gpsimd.tensor_tensor(by_batch(z2a), by_batch(z2), m2(k, A2), ALU.mult).then_inc(ln2_mod.sem, 1)
                pool.wait_ge(ln2_mod.sem, ln2_mod.after(k, "za"))
                if k:
                    pool.wait_ge(ln2_parts.sem, ln2_parts.after(k - 1, "zlo"))
                nc.gpsimd.tensor_tensor(by_batch(z2m), by_batch(z2a), m2(k, B2), ALU.add).then_inc(ln2_mod.sem, 1)
                xk = xall[:, 2 * k:2 * k + 2, :].rearrange("p b (i c) -> p b i c", i=I)
                nc.gpsimd.tensor_tensor(xk, xk, m2(k, GMB), ALU.add).then_inc(res_pool, 1)

            modulate2(0)
            keep(B - 2)
            modulate2(1)
            modulate2(2)
            keep(B - 1)
            pool.wait_ge(stat2, B * I)
            nc.gpsimd.tensor_scalar(ly2[:, EARLY:], mv2[:, EARLY:, 1], EPS, None, ALU.add).then_inc(root_pool, 1)
            pool.wait_ge(root_pool, 1)
            nc.gpsimd.tensor_tensor(y2[:, EARLY:], ly2[:, EARLY:], minus_half[:], ALU.pow).then_inc(root_pool, 1)
            modulate2(3)

        @block.scalar
        def _(act):
            act.dma_start(gqk[:, 0, :], g_q.rearrange("(o c) -> o c", o=1).broadcast_to([P, HD])).then_inc(ld_g, 16)
            act.dma_start(gqk[:, 1, :], g_k.rearrange("(o c) -> o c", o=1).broadcast_to([P, HD])).then_inc(ld_g, 16)
            act.preload_act_table_set("natural_log_exp_and_others")
            act.wait_ge(ld_c, 16)
            nc.scalar.activation(c_e[:], c_sb[:], ACT.Exp, scale=-1.0).then_inc(set_act.sem, 1)
            act.dma_start(bm_sb[:], b_mod.rearrange("(o c) -> o c", o=1).broadcast_to([B, 6 * H])).then_inc(ld_b, 16)
            act.dma_start(bias2[:, 0, :], b_proj.rearrange("(o c) -> o c", o=1).broadcast_to([B, H])).then_inc(ld_b, 16)
            act.dma_start(bias2[:, 1, :], b2.rearrange("(o c) -> o c", o=1).broadcast_to([B, H])).then_inc(ld_b, 16)
            act.wait_ge(set_dve.sem, set_dve.after(0, "eps"))

            def x_roots(S):
                act.wait_ge(S.bn, 2 * len(S.tiles))
                nc.scalar.activation(ly[:, S.of], mv[:, S.of, 1], ACT.Ln, bias=eps[:, 0:1]).then_inc(S.act.sem, 1)
                act.wait_ge(S.act.sem, S.act.after(0, "ln"))
                nc.scalar.activation(y0[:, S.of], ly[:, S.of], ACT.Exp, scale=-0.5).then_inc(S.act.sem, 1)

            x_roots(first_stats)

            def squares(b, S):
                act.wait_ge(S.qkv.sem, S.qkv.after(b, "qkv"))
                if is_later(b, S):
                    act.wait_ge(S.dve.sem, S.dve.after(b - 1, "ssum"))
                nc.scalar.activation(sq[:], ps_x[:, :, 0:2 * H], ACT.Square, scale=UNSCALE / 3.0).then_inc(S.act.sem, 1)

            def raw_out(b, S):
                if is_later(b, S):
                    act.wait_ge(S.dve.sem, S.dve.after(b - 1, "qn"))
                    act.wait_ge(v_in, b)
                nc.scalar.activation(raw[:], ps_x[:, :, 0:QKV], ACT.Copy).then_inc(S.act.sem, 1)

            def roots(b, S):
                act.wait_ge(S.dve.sem, S.dve.after(b, "ssum"))
                nc.scalar.activation(qly[:], ssum[:], ACT.Ln, bias=eps[:, 0:1]).then_inc(S.act.sem, 1)
                act.wait_ge(S.act.sem, S.act.after(b, "ln"))
                if is_later(b, S):
                    act.wait_ge(S.dve.sem, S.dve.after(b - 1, "rstd"))
                nc.scalar.activation(qy0[:], qly[:], ACT.Exp, scale=-0.5).then_inc(S.act.sem, 1)

            with act.If(needs_max(act) == 1):
                x_roots(gen_stats)
                with act.Fori(0, B) as b:
                    act.wait_ge(gen_dve.sem, gen_dve.after(b - 1, "lo"))
                    squares(b, pre)
                    raw_out(b, pre)
                    roots(b, pre)
                act.wait_ge(gen_dve.sem, gen_dve.after(B - 1, "lo"))

            squares(0, prep)
            raw_out(0, prep)
            roots(0, prep)
            x_roots(rest_stats)

            def exponentials(n, u):
                act.wait_ge(scored, n * U + u + 1)
                if is_later(n) or u >= NP:
                    act.wait_ge(summed, n * U + (u - NP + 1))
                nc.scalar.activation(pT[u % NP].rearrange("p g n -> p (g n)"),
                                     ps_s[:, 2 * (u % 2):2 * (u % 2) + 2, :].rearrange("p a n -> p (a n)"),
                                     ACT.Exp, scale=escale[:, 0:1]).then_inc(exped, 1)

            def output(n, j, par):
                act.wait_ge(summed, n * U + (2 * j + 2))
                nc.scalar.activation(oT[par][:, j, :], ps_o[:, j % 2, 0:N], ACT.Copy).then_inc(o_out, 1)

            def early_roots():
                act.wait_ge(stat2, EARLY)
                nc.scalar.activation(ly2[:, 0:EARLY], mv2[:, 0:EARLY, 1], ACT.Ln, bias=eps[:, 0:1]).then_inc(root_act.sem, 1)
                act.wait_ge(root_act.sem, root_act.after(0, "ln"))
                nc.scalar.activation(y2[:, 0:EARLY], ly2[:, 0:EARLY], ACT.Exp, scale=-0.5).then_inc(root_act.sem, 1)

            def iteration(n, par, first=False, makes=True, ahead=True):
                exponentials(n, 0)
                if makes:
                    squares(n + 1, prep)
                    raw_out(n + 1, prep)
                if not first:
                    output(n - 1, 3, 1 - par)
                if makes:
                    roots(n + 1, prep)
                exponentials(n, 1)
                if not makes:
                    early_roots()
                exponentials(n, 2)
                output(n, 0, par)
                exponentials(n, 3)
                exponentials(n, 4)
                output(n, 1, par)
                exponentials(n, 5)
                exponentials(n, 6)
                output(n, 2, par)
                exponentials(n, 7)

            iteration(0, 0, first=True)
            with act.Fori(0, (B - 4) // 2) as it:
                iteration(it * 2 + 1, 1)
                iteration(it * 2 + 2, 0)
            iteration(B - 3, 1)
            iteration(B - 2, 0, ahead=False)
            iteration(B - 1, 1, makes=False, ahead=False)
            act.preload_act_table_set("gelu_apprx_tanh_and_others")
            output(B - 1, 3, 1)

            for k in range(NB):
                for f in range(NF):
                    act.wait_ge(hid_pe, NF * k + f + 1)
                    if k >= 2:
                        act.wait_ge(y_pe, 2 * (k - 1))
                    nc.scalar.activation(hT[k % 2][0:FW[f], f, :], ps_s[0:FW[f], (NF * k + f) % 4, :],
                                         ACT.Gelu_apprx_tanh, scale=UNSCALE).then_inc(gelued, 1)

        @block.vector
        def _(dve):
            D = set_dve

            def done(name):
                dve.wait_ge(D.sem, D.after(0, name))

            nc.vector.memset(eps[:], EPS).then_inc(D.sem, 1)
            dve.wait_ge(set_act.sem, set_act.after(0, "c_e"))
            nc.vector.tensor_scalar(c_e[:], c_e[:], 1.0, None, ALU.add).then_inc(D.sem, 1)
            done("c1")
            nc.vector.reciprocal(c_s[:], c_e[:]).then_inc(D.sem, 1)
            done("c2")
            nc.vector.tensor_tensor(c_s[:], c_s[:], c_sb[:], ALU.mult).then_inc(D.sem, 1)
            dve.wait_ge(ld_g, 32)
            nc.vector.tensor_tensor(gp[:], gqk[:, 0, :], gqk[:, 1, :], ALU.mult).then_inc(D.sem, 1)
            done("gp")
            nc.vector.tensor_scalar(gneg[:], gp[:], -1.0, None, ALU.mult).then_inc(D.sem, 1)
            done("gneg")
            nc.vector.tensor_tensor(gabs[:], gp[:], gneg[:], ALU.max).then_inc(D.sem, 1)
            done("gabs")
            nc.vector.tensor_reduce(gmax[:], gabs[:], AX.X, ALU.max).then_inc(D.sem, 1)
            done("gmax")
            nc.vector.tensor_scalar(gsafe[:], gmax[:], 1e-30, None, ALU.max).then_inc(D.sem, 1)
            done("gsafe")
            nc.vector.reciprocal(ginv[:], gsafe[:]).then_inc(D.sem, 1)
            done("ginv")
            nc.vector.tensor_scalar(gbc[:], gp[:].unsqueeze(1).broadcast_to([P, NH, HD]), ginv[:, 0:1], None,
                                    ALU.mult).then_inc(D.sem, 1)
            nc.vector.tensor_scalar(escale[:], gsafe[:], 1.0 / (3.0 * QS * QS), None, ALU.mult).then_inc(D.sem, 1)
            nc.vector.tensor_scalar(flagf[:], gmax[:], SAFE_BOUND / 3.0, None, ALU.is_gt).then_inc(D.sem, 1)
            done("flagf")
            nc.vector.tensor_copy(flag[:], flagf[:]).then_inc(D.sem, 1)
            xi = xall[:].rearrange("p b (i c) -> p (b i) c", i=I)

            def x_stats(S):
                for t in S.tiles:
                    nc.vector.bn_stats(bst[:, t, :], xi[:, t, :]).then_inc(S.bn, 1)

            def x_aggregate(S):
                dve.wait_ge(S.bn, len(S.tiles))
                for t in S.tiles:
                    nc.vector.bn_aggr(mv[:, t, :], bst[:, t, :]).then_inc(S.bn, 1)

            def x_newton(S):
                dve.wait_ge(S.act.sem, S.act.after(0, "y0"))
                newton(nc, dve, S.root, 0, nt[:, S.of], y0[:, S.of], mv[:, S.of, 1], rstd[:, S.of])

            dve.wait_ge(ld_x, 16)
            x_stats(first_stats)
            dve.wait_ge(ld_id, 16)
            nc.vector.tensor_copy(id16[:], id32[:]).then_inc(D.sem, 1)
            dve.wait_ge(set_pe, 1)
            dve.wait_ge(ld_b, 48)
            nc.vector.tensor_tensor(mod[:].rearrange("b (a n) -> b a n", a=2), ps_s[0:B, 0:2, 0:3 * H],
                                    bm_sb[:].rearrange("b (a n) -> b a n", a=2), ALU.add).then_inc(D.sem, 1)
            done("mod")
            m3 = mod[:].rearrange("b (a k h) -> b a k h", a=2, k=3)
            nc.vector.tensor_scalar(mrow[:, A1:A1 + 2, :], m3[:, :, 1, :], 1.0, XS, ALU.add, ALU.mult).then_inc(D.sem, 1)
            nc.vector.tensor_scalar(mrow[:, B1:B1 + 2, :], m3[:, :, 0, :], XS, None, ALU.mult).then_inc(D.sem, 1)
            nc.vector.tensor_copy(mrow[:, GA:GA + 2, :], m3[:, :, 2, :]).then_inc(D.sem, 1)
            nc.vector.tensor_tensor(mrow[:, GAB:GAB + 2, :], m3[:, :, 2, :], bias2[:], ALU.mult).then_inc(D.sem, 1)
            x_aggregate(first_stats)
            dve.wait_ge(ld_wq, 32)
            wh = wq_f[:, :, 0:2 * H].rearrange("p c (h d) -> p c h d", d=HD)
            nc.vector.tensor_reduce(wq_m[:], wh, AX.X, ALU.add).then_inc(D.sem, 1)
            x_newton(first_stats)
            done("mean")
            nc.vector.scalar_tensor_tensor(wh, wq_m[:].unsqueeze(3).broadcast_to([KR, NC, 2 * NH, HD]), -1.0 / HD, wh,
                                           ALU.mult, ALU.add).then_inc(D.sem, 1)
            done("centred")
            nc.vector.tensor_scalar(wq_h[:], wq_f, WS, lo_row[:, 0:1], ALU.mult, ALU.mult).then_inc(D.sem, 1)
            done("wq_h")
            nc.vector.scalar_tensor_tensor(wq[:], wq_f, WS, wq_h[:], ALU.mult, ALU.subtract).then_inc(D.sem, 1)

            def stack(b, S):
                dve.wait_ge(S.pool.sem, S.pool.after(b, "xm"))
                if is_later(b, S):
                    dve.wait_ge(S.xpe.sem, S.xpe.after(b - 1, "xT"))
                xc = xm[:].rearrange("p i (c w) -> p (i c) w", w=CW)
                slots = xst[:, :, 0:3 * CW].rearrange("p t (s w) -> p t s w", w=CW)
                if not is_later(b, S):
                    dve.wait_ge(ones_set, 6)
                nc.vector.tensor_copy(slots[:, :, 0:3:2, :], xc.unsqueeze(2).broadcast_to([P, I * NC, 2, CW])
                                      ).then_inc(S.x.sem, 1)
                dve.wait_ge(S.x.sem, S.x.after(b, "xhi"))
                nc.vector.tensor_tensor(slots[:, :, 1, :], xc, slots[:, :, 0, :], ALU.subtract).then_inc(S.x.sem, 1)

            def xT_out(b, S, bank=bank16(1)):
                dve.wait_ge(S.xpe.sem, S.xpe.after(b, "xT"))
                if is_later(b, S):
                    dve.wait_ge(S.qkv.sem, S.qkv.after(b - 1, "qkv"))
                nc.vector.tensor_copy(xT[:], bank[0:KR]).then_inc(S.x.sem, 1)

            def sums(b, S):
                dve.wait_ge(S.act.sem, S.act.after(b, "sq"))
                nc.vector.tensor_reduce(ssum[:], sq[:].rearrange("p i (h d) -> p (i h) d", d=HD), AX.X, ALU.add
                                        ).then_inc(S.dve.sem, 1)

            def norm_qk(b, S):
                dve.wait_ge(S.act.sem, S.act.after(b, "y0"))
                newton(nc, dve, S.dve, b, qnt[:], qy0[:], ssum[:], qrs[:])
                dve.wait_ge(S.dve.sem, S.dve.after(b, "rstd"))
                r = qrs[:].rearrange("p (i k h) -> p i k h", i=I, k=2)
                for k, t in ((1, kn), (0, qn)):
                    if k == 0 and is_later(b, S):
                        dve.wait_ge(S.gain.sem, S.gain.after(b - 1, "qg"))
                    nc.vector.tensor_tensor(t[:].rearrange("p i (h d) -> p i h d", d=HD),
                                            raw[:, :, k * H:(k + 1) * H].rearrange("p i (h d) -> p i h d", d=HD),
                                            r[:, :, k, :].unsqueeze(3).broadcast_to([P, I, NH, HD]), ALU.mult
                                            ).then_inc(S.dve.sem, 1)

            def split_k(b, S):
                if is_later(b, S):
                    dve.wait_ge(S.pe.sem, S.pe.after(b - 1, "kT"))
                dve.wait_ge(S.dve.sem, S.dve.after(b, "kn"))
                kh = kn[:].rearrange("p i (h d) -> p (i h) d", d=HD)
                slots = kst[:, :, 0:3 * HD].rearrange("p t (s d) -> p t s d", d=HD)
                nc.vector.tensor_copy(slots[:, :, 0:2, :], kh.unsqueeze(2).broadcast_to([P, I * NH, 2, HD])
                                      ).then_inc(S.dve.sem, 1)
                dve.wait_ge(S.dve.sem, S.dve.after(b, "khi"))
                nc.vector.tensor_tensor(slots[:, :, 2, :], kh, slots[:, :, 0, :], ALU.subtract).then_inc(S.dve.sem, 1)

            def split_q(b, S):
                dve.wait_ge(S.gain.sem, S.gain.after(b, "qg"))
                qh = qg[:].rearrange("p i (h d) -> p (i h) d", d=HD)
                slots = qst[:, :, 0:3 * HD].rearrange("p t (s d) -> p t s d", d=HD)
                nc.vector.tensor_copy(slots[:, :, 0:3:2, :], qh.unsqueeze(2).broadcast_to([P, I * NH, 2, HD])
                                      ).then_inc(S.dve.sem, 1)
                dve.wait_ge(S.dve.sem, S.dve.after(b, "qhi"))
                nc.vector.tensor_tensor(slots[:, :, 1, :], qh, slots[:, :, 0, :], ALU.subtract).then_inc(S.dve.sem, 1)

            def k_out(b, S, par):
                dve.wait_ge(S.pe.sem, S.pe.after(b, "kT"))
                if S is prep and two_before(b):
                    dve.wait_ge(scored, (b - 1) * U)
                nc.vector.tensor_copy(kT[par][:], bank16(1)).then_inc(S.dve.sem, 1)

            def q_out(b, S):
                dve.wait_ge(S.pe.sem, S.pe.after(b, "qT"))
                if is_later(b, S):
                    dve.wait_ge(S.wide.sem, S.wide.after(b - 1, "g7"))
                nc.vector.tensor_copy(qP[:], bank16(0)).then_inc(S.dve.sem, 1)

            def widen(b, S, par, half):
                dve.wait_ge(S.dve.sem, S.dve.after(b, "qT"))
                if S is prep and two_before(b):
                    dve.wait_ge(scored, (b - 1) * U)
                for g in range(4):
                    rows = slice(SLOT * g, SLOT * (g + 1))
                    js = slice(JG // 2 * half, JG // 2 * (half + 1))
                    nc.vector.tensor_copy(qT[par][rows, js, g, :], qP[rows, js, :]).then_inc(S.wide.sem, 1)

            def maxima(b):
                for m in range(I * NH // 2):
                    dve.wait_ge(gen_pe, b * (I * NH // 2) + m + 1)
                    nc.vector.tensor_reduce(rmax[:, 2 * m:2 * m + 2], ps_x[:, m % 2, :].rearrange("p (h n) -> p h n", h=2),
                                            AX.X, ALU.max).then_inc(gen_max, 1)
                dve.wait_ge(gen_max, (b + 1) * (I * NH // 2))
                part = shift[:, ds(b, 1), :].rearrange("p o (t s) -> p (o t) s", s=3)
                nc.vector.tensor_scalar(sres[:], rmax[:], -1.0 / QS, None, ALU.mult).then_inc(gen_dve.sem, 1)
                for s, (name, made) in enumerate((("s0", "hi"), ("r1", "mid"), ("r2", "lo"))):
                    dve.wait_ge(gen_dve.sem, gen_dve.after(b, name))
                    nc.vector.tensor_copy(part[:, :, s], sres[:]).then_inc(gen_dve.sem, 1)
                    if s < 2:
                        dve.wait_ge(gen_dve.sem, gen_dve.after(b, made))
                        nc.vector.tensor_tensor(sres[:], sres[:], part[:, :, s], ALU.subtract).then_inc(gen_dve.sem, 1)

            with dve.If(needs_max(dve) == 1):
                x_stats(gen_stats)
                x_aggregate(gen_stats)
                x_newton(gen_stats)
                dve.wait_ge(gen_stats.root.sem, gen_stats.root.after(0, "rstd"))
                with dve.Fori(0, B) as b:
                    stack(b, pre)
                    xT_out(b, pre)
                    sums(b, pre)
                    norm_qk(b, pre)
                    split_k(b, pre)
                    split_q(b, pre)
                    k_out(b, pre, 0)
                    q_out(b, pre)
                    for half in range(2):
                        widen(b, pre, 0, half)
                    maxima(b)
                dve.wait_ge(gen_dve.sem, gen_dve.after(B - 1, "lo"))

            stack(0, prep)
            xT_out(0, prep)
            x_stats(rest_stats)
            stack(1, prep)
            sums(0, prep)
            xT_out(1, prep, first_o)
            x_aggregate(rest_stats)
            norm_qk(0, prep)
            split_k(0, prep)
            split_q(0, prep)
            x_newton(rest_stats)
            k_out(0, prep, 0)
            q_out(0, prep)
            for half in range(2):
                widen(0, prep, 0, half)

            def normalise(n):
                dve.wait_ge(post_pe.sem, post_pe.after(n, "otok"))
                ot = ps_x[:].rearrange("p i (h s) -> p (i h) s", s=SLOT)
                nc.vector.reciprocal(rden[:], ot[:, :, HD]).then_inc(post_dve.sem, 1)
                dve.wait_ge(post_dve.sem, post_dve.after(n, "rden"))
                nc.vector.tensor_tensor(o_tok[:], ot[:, :, 0:HD], rden[:].unsqueeze(2).broadcast_to([P, I * NH, HD]),
                                        ALU.mult).then_inc(post_dve.sem, 1)

            def channels(n):
                dve.wait_ge(post_pe.sem, post_pe.after(n, "och"))
                nc.vector.tensor_copy(o_ch[:], ps_x[0:HT, 0, :].rearrange("p (c n) -> p c n", c=2)).then_inc(post_dve.sem, 1)

            def projected(n):
                dve.wait_ge(post_pe.sem, post_pe.after(n, "proj"))
                nc.vector.tensor_tensor(xt[:], ps_x[:, 1, 0:I * H].rearrange("p (i c) -> p i c", i=I), mb(n, GA),
                                        ALU.mult).then_inc(gated, 1)

            def residual(n):
                dve.wait_ge(gated, n + 1)
                dve.wait_ge(biased, n + 1)
                dve.wait_ge(kept, n)
                nc.vector.tensor_tensor(x1[:], xb(n), xt[:], ALU.add).then_inc(post_dve.sem, 1)
                dve.wait_ge(post_dve.sem, post_dve.after(n, "x1"))
                for i in range(I):
                    nc.vector.bn_stats(bst2[:, i, :], x1[:, i, :]).then_inc(post_dve.sem, 1)
                dve.wait_ge(post_dve.sem, post_dve.after(n, "bn1"))
                nc.vector.tensor_copy(bst[:, ds(n * I, I), :], bst2[:]).then_inc(post_dve.sem, 1)

            def iteration(n, par, first=False, makes=True, ahead=True):
                if makes:
                    sums(n + 1, prep)
                if ahead:
                    stack(n + 2, prep)
                if makes:
                    norm_qk(n + 1, prep)
                if not first:
                    normalise(n - 1)
                if makes:
                    split_k(n + 1, prep)
                if makes:
                    split_q(n + 1, prep)
                if ahead:
                    xT_out(n + 2, prep)
                if not first:
                    channels(n - 1)
                if makes:
                    k_out(n + 1, prep, 1 - par)
                    q_out(n + 1, prep)
                if makes:
                    widen(n + 1, prep, 1 - par, 0)
                if not first:
                    projected(n - 1)
                if makes:
                    widen(n + 1, prep, 1 - par, 1)
                if not first:
                    residual(n - 1)

            iteration(0, 0, first=True)
            with dve.Fori(0, (B - 4) // 2) as it:
                iteration(it * 2 + 1, 1)
                iteration(it * 2 + 2, 0)
            iteration(B - 3, 1)
            iteration(B - 2, 0, ahead=False)

            def standardise2(k):
                if k:
                    dve.wait_ge(ln2_mod.sem, ln2_mod.after(k - 1, "za"))
                xk = xall[:, 2 * k:2 * k + 2, :].rearrange("p b (i c) -> p (b i) c", i=I)
                for t in range(T):
                    nc.vector.tensor_scalar(z2[:, t, :], xk[:, t, :], mv2[:, T * k + t, 0:1],
                                            rstd2[:, T * k + t:T * k + t + 1],
                                            ALU.subtract, ALU.mult).then_inc(ln2_z.sem, 1)

            def stack2(k):
                dve.wait_ge(ln2_mod.sem, ln2_mod.after(k, "zm"))
                if k:
                    dve.wait_ge(ln2_pe.sem, ln2_pe.after(k - 1, "zT1"))
                zc = z2m.rearrange("p t (c w) -> p (t c) w", w=CW)
                slots = zst[:, :, 0:3 * CW].rearrange("p t (s w) -> p t s w", w=CW)
                nc.vector.tensor_copy(slots[:, :, 0:3:2, :], zc.unsqueeze(2).broadcast_to([P, T * NC, 2, CW])
                                      ).then_inc(ln2_parts.sem, 1)
                dve.wait_ge(ln2_parts.sem, ln2_parts.after(k, "zhi"))
                nc.vector.tensor_tensor(slots[:, :, 1, :], zc, slots[:, :, 0, :], ALU.subtract).then_inc(ln2_parts.sem, 1)

            def zT_out(k):
                for h in range(2):
                    dve.wait_ge(ln2_pe.sem, ln2_pe.after(k, f"zT{h}"))
                    if k >= 2:
                        dve.wait_ge(hid_pe, NF * (k - 1))
                    nc.vector.tensor_copy(zT[k % 2][:, 2 * h:2 * h + 2, :], bank16(h, 2)[0:KR]).then_inc(ln2_T.sem, 1)

            def aggregate(tiles):
                dve.wait_ge(post_dve.sem, post_dve.after((tiles.stop - 1) // I, "bs"))
                for t in tiles:
                    nc.vector.bn_aggr(mv2[:, t, :], bst[:, t, :]).then_inc(stat2, 1)

            def roots(part, tiles):
                dve.wait_ge(stat2, tiles.stop)
                r = slice(tiles.start, tiles.stop)
                newton(nc, dve, root_dve, part, nt2[:, r], y2[:, r], mv2[:, r, 1], rstd2[:, r])
                dve.wait_ge(root_dve.sem, root_dve.after(part, "rstd"))

            def final(k):
                dve.wait_ge(res_pool, k + 1)
                for n in range(2):
                    dve.wait_ge(y_pe, 2 * k + n + 1)
                    if k:
                        dve.wait_ge(fin_dve.sem, fin_dve.after(k - 1, f"yo{n}"))
                    b = 2 * k + n
                    nc.vector.tensor_tensor(yg[:, n, :].rearrange("p (i c) -> p i c", i=I),
                                            ps_o[:, n, 0:I * H].rearrange("p (i c) -> p i c", i=I), mb(b, GM),
                                            ALU.mult).then_inc(fin_dve.sem, 1)
                    dve.wait_ge(fin_dve.sem, fin_dve.after(k, f"yg{n}"))
                    if k >= 2:
                        dve.wait_ge(stored[k % 2], 16 * (k // 2))
                    nc.vector.tensor_tensor(yo[k % 2][:, n, :], yg[:, n, :], xall[:, b, :], ALU.add
                                            ).then_inc(fin_dve.sem, 1)

            early, late_tiles = range(EARLY), range(EARLY, B * I)
            aggregate(early)
            normalise(B - 2)
            dve.wait_ge(root_act.sem, root_act.after(0, "y0"))
            roots(0, early)
            dve.wait_ge(kept, 2)
            standardise2(0)
            channels(B - 2)
            dve.wait_ge(w1_made, 1)
            nc.vector.scalar_tensor_tensor(w1s[:], w1_f, WS, w1_h, ALU.mult, ALU.subtract).then_inc(w1_made, 1)
            projected(B - 2)
            stack2(0)
            residual(B - 2)
            zT_out(0)
            dve.wait_ge(kept, 4)
            standardise2(1)
            normalise(B - 1)
            stack2(1)
            channels(B - 1)
            dve.wait_ge(kept, 6)
            standardise2(2)
            projected(B - 1)
            residual(B - 1)
            dve.wait_ge(w1_made, 2)
            zT_out(1)
            stack2(2)
            aggregate(late_tiles)
            dve.wait_ge(root_pool, 2)
            roots(1, late_tiles)
            final(0)
            zT_out(2)
            dve.wait_ge(kept, B)
            standardise2(3)
            stack2(3)
            final(1)
            zT_out(3)
            final(2)
            final(3)

        @block.tensor
        def _(pe):
            pe.wait_ge(ld_wm, 16)
            pe.wait_ge(set_dve.sem, set_dve.after(0, "c_s"))
            for a in range(2):
                for h in range(2):
                    mm = nc.tensor.matmul(ps_s[0:B, a, 0:3 * H], c_s[:, h, :], wm_sb[:, h, a * 3 * H:(a + 1) * 3 * H],
                                          start=(h == 0), stop=(h == 1))
            mm.then_inc(set_pe, 1)
            pe.wait_ge(set_dve.sem, set_dve.after(0, "wq"))

            def transpose_x(b, S, bank=bank16(1)):
                pe.wait_ge(S.x.sem, S.x.after(b, "xlo"))
                for c in range(NC):
                    for i in range(I):
                        tr = nc.tensor.transpose(bank[0:KR, c, i * P:(i + 1) * P], xst[:, i * NC + c, 0:KR], id16[:])
                tr.then_inc(S.xpe.sem, 1)

            def make_qkv(b, S):
                pe.wait_ge(S.x.sem, S.x.after(b, "xT"))
                for i in range(I):
                    for c in range(NC):
                        mm = nc.tensor.matmul(ps_x[:, i, 0:QKV], xT[:, c, i * P:(i + 1) * P], wq[:, c, :],
                                              start=(c == 0), stop=(c == NC - 1))
                mm.then_inc(S.qkv.sem, 1)

            def transpose_heads(b, S, st, bank):
                for j in range(JG):
                    for i in range(I):
                        tr = nc.tensor.transpose(bank16(bank)[:, j, i * P:(i + 1) * P],
                                                 st[:, i * NH + 4 * j:i * NH + 4 * j + 4, :].rearrange("p h s -> p (h s)"),
                                                 id16[:])
                tr.then_inc(S.pe.sem, 1)

            def qkv_used(b, S):
                pe.wait_ge(S.act.sem, S.act.after(b, "raw"))

            def transpose_k(b, S):
                pe.wait_ge(S.dve.sem, S.dve.after(b, "klo"))
                transpose_heads(b, S, kst, 1)

            def transpose_q(b, S):
                pe.wait_ge(S.dve.sem, S.dve.after(b, "qlo"))
                pe.wait_ge(S.gain.sem, S.gain.after(b, "sh"))
                transpose_heads(b, S, qst, 0)

            with pe.If(needs_max(pe) == 1):
                with pe.Fori(0, B) as b:
                    pe.wait_ge(gen_dve.sem, gen_dve.after(b - 1, "lo"))
                    transpose_x(b, pre)
                    make_qkv(b, pre)
                    qkv_used(b, pre)
                    transpose_k(b, pre)
                    transpose_q(b, pre)
                    pe.wait_ge(pre.dve.sem, pre.dve.after(b, "kT"))
                    pe.wait_ge(pre.wide.sem, pre.wide.after(b, "g7"))
                    for m in range(I * NH // 2):
                        if m >= 2:
                            pe.wait_ge(gen_max, b * (I * NH // 2) + (m - 1))
                        i, h = divmod(2 * m, NH)
                        for g in range(2):
                            j, r = divmod(h + g, 4)
                            mm = nc.tensor.matmul(ps_x[:, m % 2, g * N:(g + 1) * N], qT[0][:, j, r, i * P:(i + 1) * P],
                                                  kT[0][:, j, :], start=True, stop=True)
                        mm.then_inc(gen_pe, 1)
                pe.wait_ge(gen_dve.sem, gen_dve.after(B - 1, "lo"))

            transpose_x(0, prep)
            make_qkv(0, prep)
            transpose_x(1, prep, first_o)
            qkv_used(0, prep)
            transpose_k(0, prep)
            transpose_q(0, prep)

            def scores(n, u, par):
                j, i = divmod(u, 2)
                if u == 0:
                    pe.wait_ge(prep.dve.sem, prep.dve.after(n, "kT"))
                    pe.wait_ge(prep.wide.sem, prep.wide.after(n, "g3"))
                if u == 4:
                    pe.wait_ge(prep.wide.sem, prep.wide.after(n, "g7"))
                if is_later(n) or u >= 2:
                    pe.wait_ge(exped, n * U + (u - 1))
                for a in range(2):
                    mm = nc.tensor.matmul(ps_s[:, 2 * (u % 2) + a, :], kT[par][:, j, i * P:(i + 1) * P],
                                          qT[par][:, j, 2 * a:2 * a + 2, :], start=True, stop=True)
                mm.then_inc(scored, 1)

            def values(n, u, par):
                j, i = divmod(u, 2)
                if u == 0:
                    pe.wait_ge(v_in, n + 1)
                pe.wait_ge(exped, n * U + (u + 1))
                if i == 0 and (is_later(n) or j >= 2):
                    pe.wait_ge(o_out, n * JG + (j - 1))
                for g in range(4):
                    mm = nc.tensor.matmul(ps_o[SLOT * g:SLOT * (g + 1), j % 2, 0:N], v[par][:, i, 4 * j + g, :],
                                          pT[u % NP][:, g, :], start=(i == 0), stop=(i == I - 1))
                mm.then_inc(summed, 1)

            def transpose_o(n, par):
                pe.wait_ge(o_out, (n + 1) * JG)
                for i in range(I):
                    for j in range(JG):
                        tr = nc.tensor.transpose(ps_x[:, i, j * P:(j + 1) * P], oT[par][:, j, i * P:(i + 1) * P], id32[:])
                tr.then_inc(post_pe.sem, 1)

            def transpose_o_tok(n):
                pe.wait_ge(post_dve.sem, post_dve.after(n, "o"))
                ov = o_tok[:].rearrange("p (i h) d -> p i (h d)", i=I)
                for c in range(2):
                    for i in range(I):
                        tr = nc.tensor.transpose(ps_x[0:HT, 0, c * N + i * P:c * N + (i + 1) * P],
                                                 ov[:, i, c * HT:(c + 1) * HT], id32[:])
                tr.then_inc(post_pe.sem, 1)

            def project(n):
                pe.wait_ge(post_dve.sem, post_dve.after(n, "och"))
                for i in range(I):
                    for c in range(2):
                        mm = nc.tensor.matmul(ps_x[:, 1, i * H:(i + 1) * H], o_ch[:, c, i * P:(i + 1) * P], wp_sb[:, c, :],
                                              start=(c == 0), stop=(c == 1))
                mm.then_inc(post_pe.sem, 1)

            def iteration(n, par, first=False, makes=True, ahead=True):
                if not first:
                    values(n - 1, 7, 1 - par)
                scores(n, 1, par)
                values(n, 0, par)
                scores(n, 2, par)
                if makes:
                    qkv_used(n + 1, prep)
                if not first:
                    transpose_o(n - 1, 1 - par)
                values(n, 1, par)
                scores(n, 3, par)
                values(n, 2, par)
                if not first:
                    transpose_o_tok(n - 1)
                if ahead:
                    transpose_x(n + 2, prep)
                scores(n, 4, par)
                values(n, 3, par)
                scores(n, 5, par)
                if makes:
                    if ahead:
                        pe.wait_ge(prep.x.sem, prep.x.after(n + 2, "xT"))
                    else:
                        pe.wait_ge(post_dve.sem, post_dve.after(n - 1, "o"))
                    transpose_k(n + 1, prep)
                values(n, 4, par)
                if makes:
                    if not first:
                        pe.wait_ge(post_dve.sem, post_dve.after(n - 1, "och"))
                    transpose_q(n + 1, prep)
                scores(n, 6, par)
                if not first:
                    if makes:
                        pe.wait_ge(prep.dve.sem, prep.dve.after(n + 1, "kT"))
                    project(n - 1)
                values(n, 5, par)
                scores(n, 7, par)
                if makes:
                    scores(n + 1, 0, 1 - par)
                if ahead:
                    if not first:
                        pe.wait_ge(gated, n)
                    pe.wait_ge(prep.dve.sem, prep.dve.after(n + 1, "qT"))
                    make_qkv(n + 2, prep)
                values(n, 6, par)

            pe.wait_ge(ld_w, 32)
            pe.wait_ge(prep.dve.sem, prep.dve.after(0, "qT"))
            make_qkv(1, prep)
            scores(0, 0, 0)
            iteration(0, 0, first=True)
            with pe.Fori(0, (B - 4) // 2) as it:
                iteration(it * 2 + 1, 1)
                iteration(it * 2 + 2, 0)
            iteration(B - 3, 1)
            iteration(B - 2, 0, ahead=False)

            def transpose_z(k):
                pe.wait_ge(ln2_parts.sem, ln2_parts.after(k, "zlo"))
                for h in range(2):
                    if k:
                        pe.wait_ge(ln2_T.sem, ln2_T.after(k - 1, f"zT{h}"))
                    for c in range(2):
                        for t in range(T):
                            tr = nc.tensor.transpose(bank16(h, 2)[0:KR, c, t * P:(t + 1) * P],
                                                     zst[:, t * NC + 2 * h + c, 0:KR], id16[:])
                    tr.then_inc(ln2_pe.sem, 1)

            def hidden(k, tiles):
                pe.wait_ge(ln2_T.sem, ln2_T.after(k, "zT1"))
                for f in tiles:
                    m = NF * k + f
                    if m >= 4:
                        pe.wait_ge(gelued, m - 3)
                    for c in range(NC):
                        mm = nc.tensor.matmul(ps_s[0:FW[f], m % 4, :], w1s[:, c, f * FT:f * FT + FW[f]], zT[k % 2][:, c, :],
                                              start=(c == 0), stop=(c == NC - 1))
                    mm.then_inc(hid_pe, 1)

            def mlp_out(k, batches=range(2)):
                pe.wait_ge(gelued, NF * (k + 1))
                for n in batches:
                    if k:
                        pe.wait_ge(fin_dve.sem, fin_dve.after(k - 1, f"yg{n}"))
                    for i in range(I):
                        t = n * I + i
                        for f in range(NF):
                            mm = nc.tensor.matmul(ps_o[:, n, i * H:(i + 1) * H], hT[k % 2][0:FW[f], f, t * P:(t + 1) * P],
                                                  w2_sb[0:FW[f], f, :], start=(f == 0), stop=(f == NF - 1))
                    mm.then_inc(y_pe, 1)

            n, par = B - 1, 1
            values(n - 1, 7, 1 - par)
            scores(n, 1, par)
            pe.wait_ge(gated, n - 1)
            values(n, 0, par)
            scores(n, 2, par)
            transpose_o(n - 1, 1 - par)
            values(n, 1, par)
            scores(n, 3, par)
            values(n, 2, par)
            scores(n, 4, par)
            transpose_o_tok(n - 1)
            values(n, 3, par)
            scores(n, 5, par)
            values(n, 4, par)
            scores(n, 6, par)
            project(n - 1)
            values(n, 5, par)
            scores(n, 7, par)
            values(n, 6, par)
            pe.wait_ge(gated, B - 1)
            transpose_z(0)
            values(n, 7, par)
            pe.wait_ge(w1_made, 2)
            pe.wait_ge(exped, B * U)
            hidden(0, range(0, 2))
            transpose_o(n, par)
            hidden(0, range(2, 4))
            transpose_o_tok(n)
            hidden(0, range(4, NF))
            project(n)
            pe.wait_ge(o_out, B * JG)
            mlp_out(0, range(0, 1))
            pe.wait_ge(gated, B)
            transpose_z(1)
            mlp_out(0, range(1, 2))
            for k in range(1, NB):
                hidden(k, range(NF))
                if k + 1 < NB:
                    transpose_z(k + 1)
                mlp_out(k)


def newton(nc, dve, steps, b, t, y, var, result):
    nc.vector.scalar_tensor_tensor(t, y, HALF_STEP, y, ALU.mult, ALU.mult).then_inc(steps.sem, 1)
    dve.wait_ge(steps.sem, steps.after(b, "n1"))
    nc.vector.scalar_tensor_tensor(t, var, EPS, t, ALU.add, ALU.mult).then_inc(steps.sem, 1)
    dve.wait_ge(steps.sem, steps.after(b, "n2"))
    nc.vector.scalar_tensor_tensor(result, t, 1.5, y, ALU.add, ALU.mult).then_inc(steps.sem, 1)


def kernel(**inputs):
    import numpy as np
    import concourse.bacc as bacc
    from concourse.bass_utils import run_bass_kernel_spmd

    def f(name):
        return np.ascontiguousarray(np.asarray(inputs[name]))

    def stacked(w, bias):
        n = w.shape[1]
        a = np.zeros((KR, NC, n), w.dtype)
        for s in range(3):
            a[s * CW:(s + 1) * CW] = w.reshape(NC, CW, n).transpose(1, 0, 2)
        a[3 * CW:, 0] = bias
        return a

    def halves(w):
        return np.ascontiguousarray(w.reshape(2, HT, -1).transpose(1, 0, 2))

    w2 = f("L0_cond_w2")
    w2p = np.zeros((NF * FT, H), w2.dtype)
    w2p[:MLP] = w2
    lo_rows = np.zeros((KR, 1), np.float32)
    lo_rows[2 * CW:3 * CW] = 1.0
    lo_rows[KR - 1] = 1.0
    arrays = {
        "x": f("x"),
        "cT": halves(f("cond_1152").T),
        "w_mod": halves(f("L0_cond_w_mod")),
        "b_mod": f("L0_cond_b_mod"),
        "w_qkv": stacked(f("L0_cond_w_qkv"), f("L0_cond_b_qkv")),
        "g_q": f("L0_cond_g_q"),
        "g_k": f("L0_cond_g_k"),
        "w_proj": halves(f("L0_cond_w_proj")),
        "b_proj": f("L0_cond_b_proj"),
        "w1": stacked(f("L0_cond_w1"), f("L0_cond_b1")),
        "w2": np.ascontiguousarray(w2p.reshape(NF, FT, H).transpose(1, 0, 2)),
        "b2": f("L0_cond_b2"),
        "ident": np.eye(P, dtype=np.float32),
        "lo_rows": lo_rows,
    }
    nc = bacc.Bacc("TRN2", target_bir_lowering=False, num_devices=1)
    args = [nc.dram_tensor("in_" + n, a.shape, mybir.dt.from_np(a.dtype), kind="ExternalInput").ap()
            for n, a in arrays.items()]
    out = nc.dram_tensor("out", (B, N, H), F32, kind="ExternalOutput").ap()
    build(nc, *args, out)
    r = run_bass_kernel_spmd(nc, [{"in_" + n: a for n, a in arrays.items()}], core_ids=[0])
    return r.results[0]["out"]
```
